# Optimizing a Trainium2 kernel written in Bass

```python
import numpy as np
import jax
import jax.numpy as jnp

def _softmax(x, axis=-1):
    return jax.nn.softmax(x, axis=axis)

def _gelu(x):
    return jax.nn.gelu(x, approximate=True)

def _silu(x):
    return jax.nn.silu(x)

def _sigmoid(x):
    return jax.nn.sigmoid(x)

def _layernorm(x, axis=-1, eps=1e-05):
    m = jnp.mean(x, axis=axis, keepdims=True)
    v = jnp.var(x, axis=axis, keepdims=True)
    return (x - m) / jnp.sqrt(v + eps)

def _scatter_add(tgt, idx, src, axis=0):
    return tgt.at[idx].add(src)

def _segment_sum(src, seg, n):
    return jax.ops.segment_sum(src, seg, n)
kernel_name = 'mk_cond_resid_d4_seqx_r4_e90b1c'

def setup_inputs(seed: int=0):
    np.random.seed(seed)
    _w = jnp.asarray

    def _rec_inputs():
        import jax
        import jax.numpy as jnp
        _rk = jax.random.key(seed)
        x = -0.0003929 + 0.9999 * jax.random.normal(jax.random.fold_in(_rk, 1), (128, 64, 1024), jnp.float32)
        _lenS = 64 - jax.random.randint(jax.random.fold_in(_rk, 7), (128,), 0, max(1, 64 // 4) + 1, jnp.int32)
        _lenS2 = 64 - jax.random.randint(jax.random.fold_in(_rk, 8), (128,), 0, max(1, 64 // 4) + 1, jnp.int32)
        itok_B_8_3872 = jax.random.randint(jax.random.fold_in(_rk, 11), (128,), 8, 3873, jnp.int32)
        itok_B_0_15 = jax.random.randint(jax.random.fold_in(_rk, 12), (128,), 0, 16, jnp.int32)
        itok_B_6_15 = jax.random.randint(jax.random.fold_in(_rk, 13), (128,), 6, 16, jnp.int32)
        itok_B_0_2 = jax.random.randint(jax.random.fold_in(_rk, 14), (128,), 0, 3, jnp.int32)
        return (x, itok_B_8_3872, itok_B_0_15, itok_B_6_15, itok_B_0_2)
    x, itok_B_8_3872, itok_B_0_15, itok_B_6_15, itok_B_0_2 = _rec_inputs()

    def _L0_cond_setup():
        import math
        import jax, jax.numpy as jnp
        import numpy as np
        H, N, B, L = (64, 64, 16, 1024)
        DT_MIN, DT_MAX = (0.001, 0.1)

        def _get_kernel(log_dt, C, log_A_real, A_imag, length):
            Cc = C[..., 0] + 1j * C[..., 1]
            dt = jnp.exp(log_dt)
            A = -jnp.exp(log_A_real) + 1j * A_imag
            dtA = A * dt[:, None]
            P = dtA[:, :, None] * jnp.arange(length, dtype=jnp.float32)
            Cs = Cc * (jnp.exp(dtA) - 1.0) / A
            K = 2.0 * jnp.einsum('hn,hnl->hl', Cs, jnp.exp(P)).real
            return K
        key = jax.random.key(seed)
        ks = jax.random.split(key, 6)
        u = jax.random.normal(ks[0], (B, H, L), dtype=jnp.float32)
        length = jax.random.randint(ks[1], (B,), 0, L)
        log_dt = jax.random.uniform(ks[2], (H,), dtype=jnp.float32) * (math.log(DT_MAX) - math.log(DT_MIN)) + math.log(DT_MIN)
        C = jax.random.normal(ks[3], (H, N, 2), dtype=jnp.float32)
        log_A_real = jnp.log(0.5 * jnp.ones((H, N), dtype=jnp.float32))
        A_imag = math.pi * jnp.broadcast_to(jnp.arange(N, dtype=jnp.float32), (H, N))
        D = jax.random.normal(ks[4], (H,), dtype=jnp.float32)
        return {'u': u, 'length': length, 'log_dt': log_dt, 'C': C, 'log_A_real': log_A_real, 'A_imag': A_imag, 'D': D}
    _L0_cond_all = _L0_cond_setup()
    _L0_cond_in = {k: v for k, v in _L0_cond_all.items() if k in ('log_dt', 'C', 'log_A_real', 'A_imag', 'D')}
    del _L0_cond_all

    def _L1_cond_setup():
        import jax, jax.numpy as jnp
        import numpy as np
        B, C, T = (64, 64, 1024)
        S, D = (16, 64)
        key = jax.random.key(seed)
        k1, k2, k3 = jax.random.split(key, 3)
        x = jax.random.normal(k1, (B, C, T), dtype=jnp.float32)
        condition = jax.random.randint(k2, (B,), 0, S, dtype=jnp.int64)
        bound = float(np.sqrt(6.0 / C))
        weights = jax.random.uniform(k3, (S, C, D), dtype=jnp.float32, minval=-bound, maxval=bound)
        return {'x': x, 'condition': condition, 'weights': weights}
    _L1_cond_all = _L1_cond_setup()
    _L1_cond_in = {k: v for k, v in _L1_cond_all.items() if k in ('weights',)}
    del _L1_cond_all

    def _L2_cond_setup():
        import jax, jax.numpy as jnp
        import numpy as np
        B, S, D_IN, D_OUT = (4, 512, 1024, 1024)
        RANK, MAX_LORAS = (16, 32)
        key = jax.random.key(seed)
        ks = jax.random.split(key, 6)
        x = jax.random.normal(ks[0], (B, S, D_IN), dtype=jnp.float32)
        adapter_ids = jax.random.randint(ks[1], (B,), 0, MAX_LORAS)
        base_weight = jax.random.normal(ks[2], (D_OUT, D_IN), dtype=jnp.float32) * D_IN ** (-0.5)
        base_bias = jax.random.normal(ks[3], (D_OUT,), dtype=jnp.float32) * 0.01
        lora_A_w = jax.random.normal(ks[4], (MAX_LORAS, RANK, D_IN), dtype=jnp.float32) * D_IN ** (-0.5)
        lora_B_w = jax.random.normal(ks[5], (MAX_LORAS, D_OUT, RANK), dtype=jnp.float32) * RANK ** (-0.5)
        return {'x': x, 'adapter_ids': adapter_ids, 'base_weight': base_weight, 'base_bias': base_bias, 'lora_A_w': lora_A_w, 'lora_B_w': lora_B_w}
    _L2_cond_all = _L2_cond_setup()
    _L2_cond_in = {k: v for k, v in _L2_cond_all.items() if k in ('base_weight', 'base_bias', 'lora_A_w', 'lora_B_w')}
    del _L2_cond_all

    def _L3_cond_setup():
        import jax, jax.numpy as jnp
        import numpy as np
        B, S, D_IN, D_OUT = (4, 512, 1024, 1024)
        R, NUM_LABELERS = (32, 5)
        LORA_SCALING = 16 / 32
        key = jax.random.key(seed)
        k1, k2, k3, k4, k5 = jax.random.split(key, 5)
        x = jax.random.normal(k1, (B, S, D_IN), dtype=jnp.float32)
        labeler_index = jax.random.randint(k2, (B,), 0, NUM_LABELERS, dtype=jnp.int64)
        W = jax.random.normal(k3, (D_OUT, D_IN), dtype=jnp.float32) * 0.02
        lora_A = jax.random.normal(k4, (NUM_LABELERS, D_IN, R), dtype=jnp.float32) * 0.02
        lora_B_w = jax.random.normal(k5, (D_OUT, R), dtype=jnp.float32) * 0.02
        return {'x': x, 'labeler_index': labeler_index, 'W': W, 'lora_A': lora_A, 'lora_B_w': lora_B_w}
    _L3_cond_all = _L3_cond_setup()
    _L3_cond_in = {k: v for k, v in _L3_cond_all.items() if k in ('W', 'lora_A', 'lora_B_w')}
    del _L3_cond_all
    return {'x': x, 'itok_B_8_3872': itok_B_8_3872, 'itok_B_0_15': itok_B_0_15, 'itok_B_6_15': itok_B_6_15, 'itok_B_0_2': itok_B_0_2, 'L0_cond_log_dt': _L0_cond_in['log_dt'], 'L0_cond_C': _L0_cond_in['C'], 'L0_cond_log_A_real': _L0_cond_in['log_A_real'], 'L0_cond_A_imag': _L0_cond_in['A_imag'], 'L0_cond_D': _L0_cond_in['D'], 'L1_cond_weights': _L1_cond_in['weights'], 'L2_cond_base_weight': _L2_cond_in['base_weight'], 'L2_cond_base_bias': _L2_cond_in['base_bias'], 'L2_cond_lora_A_w': _L2_cond_in['lora_A_w'], 'L2_cond_lora_B_w': _L2_cond_in['lora_B_w'], 'L3_cond_W': _L3_cond_in['W'], 'L3_cond_lora_A': _L3_cond_in['lora_A'], 'L3_cond_lora_B_w': _L3_cond_in['lora_B_w']}

def reference(x, itok_B_8_3872, itok_B_0_15, itok_B_6_15, itok_B_0_2, L0_cond_log_dt, L0_cond_C, L0_cond_log_A_real, L0_cond_A_imag, L0_cond_D, L1_cond_weights, L2_cond_base_weight, L2_cond_base_bias, L2_cond_lora_A_w, L2_cond_lora_B_w, L3_cond_W, L3_cond_lora_A, L3_cond_lora_B_w):
    import jax
    import jax.numpy as jnp

    def _L0_cond_ref(u, length, log_dt, C, log_A_real, A_imag, D):
        import math
        import jax, jax.numpy as jnp
        import numpy as np
        H, N, B, L = (64, 64, 16, 1024)
        DT_MIN, DT_MAX = (0.001, 0.1)

        def _get_kernel(log_dt, C, log_A_real, A_imag, length):
            Cc = C[..., 0] + 1j * C[..., 1]
            dt = jnp.exp(log_dt)
            A = -jnp.exp(log_A_real) + 1j * A_imag
            dtA = A * dt[:, None]
            P = dtA[:, :, None] * jnp.arange(length, dtype=jnp.float32)
            Cs = Cc * (jnp.exp(dtA) - 1.0) / A
            K = 2.0 * jnp.einsum('hn,hnl->hl', Cs, jnp.exp(P)).real
            return K
        Bq, Hq, Lq = u.shape
        mask = (jnp.arange(Lq) < length[:, None]).astype(u.dtype)
        u_m = u * mask[:, None, :]
        kernel = _get_kernel(log_dt, C, log_A_real, A_imag, Lq)
        n = 2 * Lq
        k_f = jnp.fft.rfft(kernel, n=n)
        u_f = jnp.fft.rfft(u_m, n=n)
        y = jnp.fft.irfft(u_f * k_f, n=n)[..., :Lq]
        y = y + u_m * D[:, None]
        return y * mask[:, None, :]

    def _L1_cond_ref(x, condition, weights):
        import jax, jax.numpy as jnp
        import numpy as np
        B, C, T = (64, 64, 1024)
        S, D = (16, 64)
        W = weights[condition]
        return jnp.einsum('bct,bcd->bdt', x, W)

    def _L2_cond_ref(x, adapter_ids, base_weight, base_bias, lora_A_w, lora_B_w):
        import jax, jax.numpy as jnp
        import numpy as np
        B, S, D_IN, D_OUT = (4, 512, 1024, 1024)
        RANK, MAX_LORAS = (16, 32)
        result = jnp.einsum('bsd,od->bso', x, base_weight) + base_bias
        A = lora_A_w[adapter_ids]
        Bw = lora_B_w[adapter_ids]
        h = jnp.einsum('bsd,brd->bsr', x, A)
        lora_out = jnp.einsum('bsr,bor->bso', h, Bw)
        result = result + lora_out
        return result.astype(x.dtype)

    def _L3_cond_ref(x, labeler_index, W, lora_A, lora_B_w):
        import jax, jax.numpy as jnp
        import numpy as np
        B, S, D_IN, D_OUT = (4, 512, 1024, 1024)
        R, NUM_LABELERS = (32, 5)
        LORA_SCALING = 16 / 32
        base = jnp.einsum('bsi,oi->bso', x, W)
        labelers_A = lora_A[labeler_index]
        low = jnp.einsum('bsi,bir->bsr', x, labelers_A)
        delta = jnp.einsum('bsr,or->bso', low, lora_B_w) * LORA_SCALING
        return base + delta
    x = x + _L0_cond_ref(x, itok_B_8_3872, L0_cond_log_dt, L0_cond_C, L0_cond_log_A_real, L0_cond_A_imag, L0_cond_D)
    x = x + _L1_cond_ref(x, itok_B_0_15, L1_cond_weights)
    x = x + _L2_cond_ref(x, itok_B_6_15, L2_cond_base_weight, L2_cond_base_bias, L2_cond_lora_A_w, L2_cond_lora_B_w)
    x = x + _L3_cond_ref(x, itok_B_0_2, L3_cond_W, L3_cond_lora_A, L3_cond_lora_B_w)
    return x

_drawn_inputs = setup_inputs


def setup_inputs(seed=0):
    import zlib

    import numpy as np

    out = dict(_drawn_inputs(seed))
    spreads = {'L0_cond_log_A_real': (-0.6931471824645996, 0.2)}
    factors = {'L2_cond_base_bias': 38.274}
    for name, (base, spread) in spreads.items():
        noise = np.random.default_rng([zlib.crc32(name.encode()), seed]).standard_normal(out[name].shape)
        drawn = base * np.exp(spread * noise) if base else spread * noise
        out[name] = jnp.asarray(drawn.astype(out[name].dtype))
    for name, factor in factors.items():
        out[name] = (out[name] * factor).astype(out[name].dtype)
    return out
```

```python
import math

import concourse.bass as bass
from concourse import mybir

F32, F32R = mybir.dt.float32, mybir.dt.float32r
I32, U8 = mybir.dt.int32, mybir.dt.uint8
ALU = mybir.AluOpType
ACT = mybir.ActivationFunctionType

B, C, T = 128, 64, 1024
N = 64
P = 128
K8 = T // P
S1 = 16
A2N, R2 = 32, 16
L3N, R3 = 5, 32
AR, LR = A2N * R2, L3N * R3
G = 32
HB = T // 2
TILES = B // 2
KR = 2 * R2 + 2 * R3
ROUND = 1.5 * 2.0 ** 23
TWO_PI = 6.283184
LOG2E = 1.4426950408889634
LN2_HI, LN2_LO = 0.693145751953125, 1.4286068203094172e-06
LAYOUT_END = 229368


def program(nc, x, steps, cond, adapter, labeler, log_dt, ssm_c, log_a_real, a_imag, ssm_d,
            mix_w, w2, bias2, lora2_a, lora2_b, w3, lora3_a, lora3_b, out):
    base = (nc.sbuf_base + 63) // 64 * 64

    def at(name, shape, dtype, offset):
        size = math.prod(shape[1:]) * mybir.dt.size(dtype)
        assert base + offset + size <= LAYOUT_END, (name, base + offset + size)
        return nc.alloc_sbuf_tensor_at(name, shape, dtype, offset=base + offset), (offset + size + 31) // 32 * 32

    half_t = K8 // 2
    dense0, o_dense1 = at("dense0", [P, 2, half_t, T], F32R, 0)
    dense1, o_lora_in = at("dense1", [P, 2, half_t, T], F32R, o_dense1)
    lora_in, o_mix = at("lora_in", [P, 2, K8, AR + LR], F32R, o_lora_in)
    mix, o_b3s = at("mix", [P, 2, S1, C], F32R, o_mix)
    b3s, o = at("b3s", [P, 2, T], F32R, o_b3s)
    ident, o = at("ident", [P, P], F32, o)
    index, o = at("index", [1, 3 * B], I32, o)
    mask, o_phase = at("mask", [P, T], U8, o)

    lora_a_raw, o_nat = at("lora_a_raw", [P, AR // P, T], F32, 0)
    o = o_dense1
    fac_u, o = at("fac_u", [P, C, G], F32, o)
    fac_v, o = at("fac_v", [P, C, G], F32, o)
    fac_w, o_fac_t = at("fac_w", [P, C, G], F32, o)
    fac_t, o = at("fac_t", [P, C, G], F32, o_fac_t)
    kern, _ = at("kern", [G, C, G], F32, o_fac_t)
    ramp, _ = at("ramp", [P, T], F32, o_fac_t)
    w3_raw, o = at("w3_raw", [P, K8, T], F32, o_lora_in)
    assert o <= o_mix
    p2, o_p3 = at("p2", [P, K8, T], F32, o_phase)
    p3, o_b2 = at("p3", [P, K8, T], F32, o_p3)
    b2raw, o_a3 = at("b2raw", [P, K8, AR], F32, o_b2)
    a3raw, o = at("a3raw", [P, K8, LR], F32, o_a3)
    bias_col, o_diag = at("bias_col", [P, K8], F32, o)
    diag, o_x01 = at("diag", [P, T + K8], F32, o_diag)
    ct, o = at("ct", [P, 2, AR + 1], F32, o_diag)
    assert o <= o_x01
    b3rep, o = at("b3rep", [P, K8, 4, R3], F32, o_x01)
    part, o = at("part", [P, 4, C], F32, o)
    grid, o = at("grid", [P, 2, G], F32, o)
    phase, o = at("phase", [P, 6], F32, o)
    last, o = at("last", [G, 1], F32, o)
    dcol, o = at("dcol", [G, C], F32, o)
    par, o = at("par", [C, 4 * 2 * N], F32, o)
    assert o <= o_x01 + 2 * 4 * T
    o = o_phase
    b2p, o = at("b2p", [P, AR // P, T], F32, o)
    b2p_bias, o = at("b2p_bias", [1, T], F32, o)
    fold0, o = at("fold0", [P, T], F32, o)
    fold1, o = at("fold1", [P, T], F32, o)
    b3t, o = at("b3t", [P, T], F32, o)
    fold = [fold0, fold1]
    assert o <= o_p3
    b2s, o = [], o_p3
    for i in range(4):
        t, o = at(f"b2s{i}", [P, 2, T], F32R, o)
        b2s.append(t)
    assert o <= o_b2

    o = o_nat
    def nat(name, cols, dtype=F32, parts=C):
        nonlocal o
        t, o = at(name, [parts, cols], dtype, o)
        return t
    logs, exps = nat("logs", N + 1), nat("exps", N + 1)
    e_k, e_f, e_q, e_2k = (nat(f"e_{n}", N + 1) for n in "kfqs")
    e_i = nat("e_i", N + 1, I32)
    aim, cri = nat("aim", N), nat("cri", 2 * N)
    decay, angle, em1, turns, frac, sin1, sinh, cosm1, zr, zi, den, nr, ni, tmp, tmp2 = (
        nat(f"n_{n}", N) for n in range(15))
    lens_i, lens = nat("lens_i", 1, I32, P), nat("lens", 1, parts=P)
    mraw, mtmp = nat("mraw", S1 * C, parts=P), nat("mtmp", S1 * C, parts=P)
    zero = nat("zero", P)
    assert o <= o_dense1, o - o_dense1

    ut, toep, toep_raw, xt = [], [], [], []
    o = o_p3
    for i in range(2):
        t, o = at(f"ut{i}", [P, 2, K8, P], F32R, o)
        ut.append(t)
    for i in range(2):
        t, o = at(f"toep{i}", [P, 2, T], F32R, o)
        toep.append(t)
    assert o <= o_b2
    o = o_b2
    for i in range(2):
        t, o = at(f"toep_raw{i}", [P, T], F32, o)
        toep_raw.append(t)
    o_x23, o = o, o_x01
    for i in range(2):
        t, o = at(f"xt{i}", [P, T], F32, o)
        xt.append(t)
    o = o_x23
    for i in range(2, 4):
        t, o = at(f"xt{i}", [P, T], F32, o)
        xt.append(t)
    assert o <= o_a3

    o = o_phase
    def pair(name, shape, dtype):
        nonlocal o
        two = []
        for i in range(2):
            t, o = at(f"{name}{i}", shape, dtype, o)
            two.append(t)
        return two
    x1_in = pair("x1_in", [P, T], F32)
    x1s = pair("x1s", [P, 2, T], F32R)
    x2t = pair("x2t", [P, 2, K8, P], F32R)
    y_out = pair("y_out", [P, T], F32)
    a_gath = pair("a_gath", [P, 2, K8, KR], F32R)
    m_gath = pair("m_gath", [P, 2, P], F32R)
    stack = pair("stack", [KR + 2, 2, T], F32R)
    hs = pair("hs", [KR + 2, 2, P], F32R)
    hm = pair("hm", [KR, P], F32)
    hmask, o = at("hmask", [KR + 2, P], F32, o)

    ps = [nc.alloc_psum_tensor(f"ps{i}", [P, T], F32) for i in range(4)]
    kern_d = nc.dram_tensor("kern_d", [C, T + P], F32).ap()
    x1_d = nc.dram_tensor("x1_d", [B, C, T], F32).ap()
    b2_d = nc.dram_tensor("b2_d", [L3N * A2N, R2, 2, T], F32).ap()
    row_d = nc.dram_tensor("row_d", [L3N, 1, 2, T], F32).ap()

    def f(ap):
        return ap.bitcast(F32)

    J_PAR = 0
    J_W3 = J_PAR + 1
    J_LA = J_W3 + K8
    J_D0 = J_LA + K8
    J_K = J_D0 + half_t
    J_D1 = J_K + 2
    J_A3 = J_D1 + half_t
    J_C = J_A3 + K8
    J_B2 = J_C + 2
    J_B3 = J_B2 + AR // P + 1
    J_F = J_B3 + 1
    CONSTS, FIXED = 7 + 12 + 3, 16
    FOLDS = [(l, m) for l in range(L3N) for m in range(AR // P + 1)]
    JOBS = J_F + len(FOLDS)

    sem = nc.alloc_semaphore
    in_small, in_w3, in_la, in_w2, in_lb, in_mix = (sem(f"in_{n}") for n in ("small", "w3", "la", "w2", "lb", "mix"))
    consts = sem("consts")
    chain = sem("chain")
    pchain = sem("pchain")
    base_ready = sem("base_ready")
    trig_in, trig_out = sem("trig_in"), sem("trig_out")
    fac_in, fac_out = sem("fac_in"), sem("fac_out")
    factors = sem("factors")
    p2_ready = sem("p2_ready")
    job_done, job_hi, job_free = sem("job_done"), sem("job_hi"), sem("job_free")
    kern_ready, kern_stored = sem("kern_ready"), sem("kern_stored")
    fold_sum, fold_hi, fold_lo = (sem(f"fold_{n}") for n in ("sum", "hi", "lo"))
    fold_stored = [sem(f"fold_stored{i}") for i in range(4)]
    mix_ready = sem("mix_ready")
    b3_ready = sem("b3_ready")


    def ready(eng, semaphore, value):
        if not isinstance(value, int) or value > 0:
            eng.wait_ge(semaphore, value)

    x_in = [sem(f"x_in{i}") for i in range(4)]
    x1_stored = [sem(f"x1_stored{i}") for i in range(4)]
    toep_in = [sem(f"toep_in{i}") for i in range(2)]
    toep_hi, toep_lo = sem("toep_hi"), sem("toep_lo")
    ut_ps, ut_hi, ut_lo = sem("ut_ps"), sem("ut_hi"), sem("ut_lo")
    conv_done, x1_ready = sem("conv_done"), sem("x1_ready")
    mask_begun = sem("mask_begun")
    GROUPS = C // 4

    def over_channels(eng, body):
        for u in range(4):
            body(0, u)
        with eng.Fori(1, GROUPS) as k:
            for u in range(4):
                body(k, u)

    toep_view = bass.AP(tensor=kern_d.tensor, offset=0, ap=[[T + P, C], [1, P], [1, T]])
    b2_rows = b2_d.rearrange("a r h t -> (a r) h t")

    with nc.Block() as block:
        @block.sync
        def _(sp):
            for to, of in ((logs[:, 0:N], log_a_real), (logs[:, N:N + 1], log_dt.unsqueeze(1)),
                           (aim[:], a_imag), (cri[:], ssm_c.rearrange("h n c -> h (n c)")),
                           (dcol[:], ssm_d.unsqueeze(0).to_broadcast([G, C])),
                           (lens_i[:], steps.unsqueeze(1)),
                           (index[:, 0:B], cond.unsqueeze(0)), (index[:, B:2 * B], adapter.unsqueeze(0)),
                           (index[:, 2 * B:3 * B], labeler.unsqueeze(0))):
                sp.dma_start(to, of).then_inc(in_small, 16)
            sp.dma_start(w3_raw[:], w3.rearrange("(c p) d -> p c d", p=P)).then_inc(in_w3, 16)
            sp.dma_start(lora_a_raw[:], lora2_a.rearrange("(c a) r t -> (a r) c t", c=AR // P)).then_inc(in_la, 16)
            for half in range(2):
                sp.dma_start(mraw[C * half:C * half + C, :].rearrange("p (s d) -> p s d", s=S1),
                             mix_w.rearrange("s c d -> c s d")).then_inc(in_mix, 16)
            sp.dma_start(p2[:], w2.rearrange("(p i) t -> p i t", i=K8)).then_inc(in_w2, 16)
            for i in range(K8):
                sp.dma_start(b2raw[:, i, :].rearrange("p (a r) -> p a r", r=R2),
                             lora2_b.rearrange("a (p i) r -> i p a r", i=K8)[i]).then_inc(in_lb, 16)
                sp.dma_start(a3raw[:, i, :].rearrange("p (l r) -> p l r", r=R3),
                             lora3_a.rearrange("l (p i) r -> i p l r", i=K8)[i]).then_inc(in_lb, 16)
            sp.dma_start(bias_col[:], bias2.rearrange("(p i) -> p i", i=K8)).then_inc(in_lb, 16)
            for rep in range(4):
                sp.dma_start(b3rep[:, :, rep, :], lora3_b.rearrange("(c p) r -> p c r", p=P)).then_inc(in_lb, 16)

            sp.wait_ge(consts, 7)
            sp.dma_start(kern_d[:, T:T + P], zero[:]).then_inc(kern_stored, 16)
            sp.wait_ge(kern_ready, 1)
            sp.dma_start(kern_d[:, 0:T].rearrange("h (q r) -> q h r", q=G), kern[:]).then_inc(kern_stored, 16)

            def load_x(k, u):
                if not isinstance(k, int) or k > 0:
                    sp.wait_ge(x1_stored[u], 16 * k)
                sp.dma_start(xt[u][:], x[:, bass.ds(4 * k + u, 1), :].squeeze(1)).then_inc(x_in[u], 16)

            def load_toep(k, u):
                h = 4 * k + u
                ready(sp, toep_hi, h - 1)
                ready(sp, toep_lo, h - 1)
                sp.dma_start(toep_raw[u % 2][:], toep_view[bass.ds(h, 1), :, :].squeeze(0)).then_inc(toep_in[u % 2], 16)

            def store_x1(k, u):
                sp.wait_ge(x1_ready, 4 * k + u + 1)
                sp.dma_start(x1_d[:, bass.ds(4 * k + u, 1), :].squeeze(1), xt[u][:]).then_inc(x1_stored[u], 16)

            sp.wait_ge(kern_stored, 32)
            sp.wait_ge(job_done, J_B3 + 1)
            for u in range(3):
                load_x(0, u)
            for u in range(2):
                load_toep(0, u)

            for s, (l, m) in enumerate(FOLDS):
                sp.wait_ge(fold_lo, s + 1)
                if m < AR // P:
                    sp.dma_start(b2_rows[l * AR + m * P:l * AR + (m + 1) * P], f(b2s[s % 4][:])).then_inc(fold_stored[s % 4], 16)
                else:
                    sp.dma_start(row_d[l], f(b2s[s % 4][0:1])).then_inc(fold_stored[s % 4], 16)

            def channel(k, u, loads=True):
                if loads or u < 1:
                    load_x(k + (u + 3) // 4, (u + 3) % 4)
                if loads or u < 2:
                    load_toep(k + (u + 2) // 4, (u + 2) % 4)
                store_x1(k, u)

            for u in range(4):
                channel(0, u)
            with sp.Fori(1, GROUPS - 1) as k:
                for u in range(4):
                    channel(k, u)
            for u in range(4):
                channel(GROUPS - 1, u, loads=False)
            for u in range(4):
                sp.wait_ge(x1_stored[u], 16 * GROUPS)

        @block.gpsimd
        def _(pool):
            made = [0]

            def const(ins):
                made[0] += 1
                ins.then_inc(consts, 1)
                pool.wait_ge(consts, made[0])

            const(nc.gpsimd.memset(ident[:], 0.0))
            const(nc.gpsimd.affine_select(ident[:], ident[:], pattern=[[-1, P]], base=0, channel_multiplier=1,
                                          compare_op=ALU.not_equal, fill=1.0))
            const(nc.gpsimd.iota(grid[:, 0, :], pattern=[[-G, G]], base=G * (G - 1), channel_multiplier=0,
                                 allow_small_or_imprecise_dtypes=True))
            const(nc.gpsimd.iota(grid[:, 1, :], pattern=[[-1, G]], base=G - 1, channel_multiplier=0,
                                 allow_small_or_imprecise_dtypes=True))
            const(nc.gpsimd.memset(last[:], 0.0))
            const(nc.gpsimd.affine_select(last[:], last[:], pattern=[[0, 1]], base=1 - G, channel_multiplier=1,
                                          compare_op=ALU.not_equal, fill=1.0))
            const(nc.gpsimd.memset(zero[:], 0.0))
            for half, turns3 in enumerate(((0.25, 0.5, 0.25), (0.5, 0.75, 0.0))):
                for j, turn in enumerate(turns3):
                    const(nc.gpsimd.memset(phase[64 * half:64 * half + 64, j:j + 1], turn))
                    const(nc.gpsimd.memset(phase[64 * half:64 * half + 64, 3 + j:4 + j], turn * TWO_PI))
            const(nc.gpsimd.iota(ramp[:], pattern=[[1, T]], base=0, channel_multiplier=0,
                                 allow_small_or_imprecise_dtypes=True))
            const(nc.gpsimd.memset(diag[:], 0.0))
            const(nc.gpsimd.affine_select(diag[:], diag[:], pattern=[[1, T + K8]], base=-(K8 - 1), channel_multiplier=-K8,
                                          compare_op=ALU.not_equal, fill=1.0))
            assert made[0] == CONSTS

            steps_done = [0]

            def link(ins):
                steps_done[0] += 1
                ins.then_inc(pchain, 1)
                pool.wait_ge(pchain, steps_done[0])

            pool.wait_ge(in_mix, 32)
            m3 = mraw[:].rearrange("p (s d) -> p s d", s=S1)
            for half in range(2):
                rows = slice(C * half, C * half + C)
                link(nc.gpsimd.tensor_tensor(mtmp[rows, :].rearrange("p (s d) -> p s d", s=S1), m3[rows],
                                             ident[rows, C * half:C * half + C].unsqueeze(1).to_broadcast([C, S1, C]), ALU.add))
            t3 = mtmp[:].rearrange("p (s d) -> p s d", s=S1)
            link(nc.gpsimd.tensor_copy(mix[:, 0], t3))
            link(nc.gpsimd.tensor_tensor(mix[:, 1], t3, f(mix[:, 0]), ALU.subtract))

            pool.wait_ge(in_w2, 16)
            for i in range(K8):
                last_add = nc.gpsimd.tensor_tensor(p2[:, i, :], p2[:, i, :], diag[:, K8 - 1 - i:K8 - 1 - i + T], ALU.add)
            last_add.then_inc(p2_ready, 1)

            for s, (l, m) in enumerate(FOLDS):
                rows = P if m < AR // P else 1
                pool.wait_ge(fold_hi, s + 1)
                nc.gpsimd.tensor_tensor(b2s[s % 4][0:rows, 1], fold[s % 2][0:rows, :], f(b2s[s % 4][0:rows, 0]),
                                        ALU.subtract).then_inc(fold_lo, 1)

            def toep_low(k, u):
                h = 4 * k + u
                pool.wait_ge(toep_hi, h + 1)
                nc.gpsimd.tensor_tensor(toep[u % 2][:, 1], toep_raw[u % 2][:, ::-1], f(toep[u % 2][:, 0]),
                                        ALU.subtract).then_inc(toep_lo, 1)

            over_channels(pool, toep_low)

        @block.scalar
        def _(act):
            def trig(k, to, of, func, scale, bias=0.0, signal=trig_out):
                nc.scalar.activation(to, of, func, scale=scale, bias=bias).then_inc(signal, 1)

            act.wait_ge(trig_in, 1)
            nc.scalar.activation(sin1[:], frac[:], ACT.Sin, scale=TWO_PI).then_inc(trig_out, 1)
            nc.scalar.activation(sinh[:], frac[:], ACT.Sin, scale=TWO_PI / 2).then_inc(trig_out, 1)
            act.wait_ge(fac_in, 1)
            nc.scalar.activation(fac_t[:], fac_t[:], ACT.Exp).then_inc(fac_out, 1)
            act.wait_ge(fac_in, 2)
            nc.scalar.activation(fac_u[:], fac_u[:], ACT.Sin, scale=-TWO_PI, bias=phase[:, 3:4]).then_inc(fac_out, 1)
            act.wait_ge(fac_in, 3)
            nc.scalar.activation(fac_w[:], fac_w[:], ACT.Sin, scale=-TWO_PI, bias=phase[:, 4:5]).then_inc(fac_out, 1)
            act.wait_ge(fac_in, 4)
            nc.scalar.activation(fac_w[:], fac_w[:], ACT.Sin, scale=-TWO_PI, bias=phase[:, 5:6]).then_inc(fac_out, 1)
            act.wait_ge(fac_in, 5)
            nc.scalar.activation(fac_t[:], fac_t[:], ACT.Exp).then_inc(fac_out, 1)

            def high(j, to, of):
                act.wait_ge(job_done, j + 1)
                nc.scalar.activation(to, of, ACT.Copy).then_inc(job_hi, 1)

            for i in range(K8):
                high(J_LA + i, lora_in[:, 0, i, 0:AR], ps[(J_LA + i) % 4][:, 0:AR])
            act.wait_ge(factors, 1)
            act.wait_ge(kern_stored, 16)
            act.wait_ge(pchain, 4)
            for i in range(half_t):
                high(J_D0 + i, dense0[:, 0, i, :], ps[(J_D0 + i) % 4][:])
            act.wait_ge(kern_stored, 32)
            for i in range(half_t):
                high(J_D1 + i, dense1[:, 0, i, :], ps[(J_D1 + i) % 4][:])
            for i in range(K8):
                high(J_A3 + i, lora_in[:, 0, i, AR:AR + LR], ps[(J_A3 + i) % 4][:, 0:LR])
            act.wait_ge(b3_ready, 1)
            nc.scalar.activation(b3s[:, 0], b3t[:], ACT.Copy).then_inc(b3_ready, 1)
            for s, (l, m) in enumerate(FOLDS):
                rows = P if m < AR // P else 1
                act.wait_ge(fold_sum, s + 1)
                if s >= 4:
                    act.wait_ge(fold_stored[s % 4], 16 * (s // 4))
                nc.scalar.activation(b2s[s % 4][0:rows, 0], fold[s % 2][0:rows, :], ACT.Copy).then_inc(fold_hi, 1)
            for i in range(4):
                act.wait_ge(fold_stored[i], 16 * len(FOLDS[i::4]))

            def split_high(k, u):
                h = 4 * k + u
                act.wait_ge(toep_in[u % 2], 32 * k + 16 * (u // 2) + 16)
                ready(act, conv_done, h - 1)
                nc.scalar.activation(toep[u % 2][:, 0], toep_raw[u % 2][:, ::-1], ACT.Copy).then_inc(toep_hi, 1)
                act.wait_ge(ut_ps, h + 1)
                nc.scalar.activation(ut[u % 2][:, 0], ps[u % 2][:].rearrange("p (i b) -> p i b", i=K8),
                                     ACT.Copy).then_inc(ut_hi, 1)

            over_channels(act, split_high)

        @block.vector
        def _(dve):
            count = [0]

            def link(ins):
                count[0] += 1
                ins.then_inc(chain, 1)
                dve.wait_ge(chain, count[0])

            tt, ts, stt = nc.vector.tensor_tensor, nc.vector.tensor_scalar, nc.vector.scalar_tensor_tensor

            def exp_parts(z, k, r, q, two_k, ki):
                link(ts(k, z, LOG2E, ROUND, ALU.mult, ALU.add))
                link(ts(k, k, ROUND, -126.0, ALU.subtract, ALU.max))
                link(ts(k, k, 127.0, None, ALU.min))
                link(stt(r, k, -LN2_HI, z, ALU.mult, ALU.add))
                link(stt(r, k, -LN2_LO, r, ALU.mult, ALU.add))
                link(ts(q, r, 1.0 / 40320, None, ALU.mult))
                for n in (5040, 720, 120, 24, 6, 2, 1):
                    link(stt(q, q, 1.0 / n, r, ALU.add, ALU.mult))
                link(ts(ki, k, 127.0, None, ALU.add))
                link(ts(two_k.bitcast(I32), ki, 23, None, ALU.logical_shift_left))

            dve.wait_ge(in_small, 16 * 9)
            exp_parts(logs[:], e_k[:], e_f[:], e_q[:], e_2k[:], e_i[:])
            link(tt(e_q[:], e_q[:], e_2k[:], ALU.mult))
            link(tt(exps[:], e_q[:], e_2k[:], ALU.add))
            ar, dt = exps[:, 0:N], exps[:, N:N + 1]
            link(ts(decay[:], ar, dt, -1.0, ALU.mult, ALU.mult))
            link(ts(angle[:], aim[:], dt, None, ALU.mult))
            link(ts(turns[:], angle[:], 1.0 / (2 * math.pi), None, ALU.mult))
            link(ts(tmp[:], turns[:], ROUND, ROUND, ALU.add, ALU.subtract))
            dve.wait_ge(chain, count[0])
            tt(frac[:], turns[:], tmp[:], ALU.subtract).then_inc(trig_in, 1)
            exp_parts(decay[:], e_k[:, 0:N], e_f[:, 0:N], e_q[:, 0:N], e_2k[:, 0:N], e_i[:, 0:N])
            link(tt(e_q[:, 0:N], e_q[:, 0:N], e_2k[:, 0:N], ALU.mult))
            link(ts(e_f[:, 0:N], e_2k[:, 0:N], 1.0, None, ALU.subtract))
            link(tt(em1[:], e_q[:, 0:N], e_f[:, 0:N], ALU.add))
            dve.wait_ge(trig_out, 2)
            link(tt(tmp[:], sinh[:], sinh[:], ALU.mult))
            link(ts(cosm1[:], tmp[:], -2.0, None, ALU.mult))
            link(stt(zr[:], cosm1[:], 1.0, em1[:], ALU.add, ALU.mult))
            link(tt(zr[:], zr[:], cosm1[:], ALU.add))
            link(stt(zi[:], em1[:], 1.0, sin1[:], ALU.add, ALU.mult))
            link(tt(tmp[:], ar, ar, ALU.mult))
            link(tt(den[:], aim[:], aim[:], ALU.mult))
            link(tt(den[:], den[:], tmp[:], ALU.add))
            link(nc.vector.reciprocal(den[:], den[:]))
            link(tt(nr[:], zi[:], aim[:], ALU.mult))
            link(tt(tmp[:], zr[:], ar, ALU.mult))
            link(tt(nr[:], nr[:], tmp[:], ALU.subtract))
            link(stt(nr[:], nr[:], 2.0, den[:], ALU.mult, ALU.mult))
            link(tt(ni[:], zr[:], aim[:], ALU.mult))
            link(tt(tmp[:], zi[:], ar, ALU.mult))
            link(tt(ni[:], ni[:], tmp[:], ALU.add))
            link(stt(ni[:], ni[:], -2.0, den[:], ALU.mult, ALU.mult))
            c3 = cri[:].rearrange("h (n c) -> h n c", c=2)
            p4 = par[:].rearrange("h (j d n) -> h j d n", j=4, d=2)
            def both(j):
                return p4[:, j, :, :]
            def twice(t):
                return t[:].unsqueeze(1).to_broadcast([C, 2, N])
            link(nc.vector.tensor_copy(both(0), twice(decay)))
            link(nc.vector.tensor_copy(both(1), twice(turns)))
            link(tt(tmp[:], nr[:], c3[:, :, 0], ALU.mult))
            link(tt(tmp2[:], ni[:], c3[:, :, 1], ALU.mult))
            link(tt(both(2), twice(tmp), twice(tmp2), ALU.subtract))
            link(tt(tmp[:], nr[:], c3[:, :, 1], ALU.mult))
            link(tt(tmp2[:], ni[:], c3[:, :, 0], ALU.mult))
            link(tt(both(3), twice(tmp), twice(tmp2), ALU.add))
            nc.vector.tensor_copy(lens[:], lens_i[:]).then_inc(base_ready, 1)
            dve.wait_ge(base_ready, 1)
            dve.wait_ge(consts, CONSTS)
            link(ts(mask[:], ramp[:], lens[:], None, ALU.is_lt))
            mask_made = count[0]
            dve.wait_ge(job_done, J_PAR + 1)
            link(nc.vector.tensor_copy(part[:], ps[0][:, 0:4 * C].rearrange("p (j h) -> p j h", j=4)))
            nc.vector.tensor_copy(tmp[:, 0:1], lens[0:C, :]).then_inc(job_free, 1)

            def across(j):
                return part[:, j, :].unsqueeze(2).to_broadcast([P, C, G])

            def steps_of(j):
                return grid[:, j, :].unsqueeze(1).to_broadcast([P, C, G])

            tt(fac_t[:], across(0), steps_of(0), ALU.mult).then_inc(fac_in, 1)
            link(tt(fac_v[:], across(1), steps_of(0), ALU.mult))
            link(ts(fac_u[:], fac_v[:], phase[:, 0:1], ROUND, ALU.add, ALU.add))
            stt(fac_u[:], fac_u[:], ROUND, fac_v[:], ALU.subtract, ALU.subtract).then_inc(fac_in, 1)
            link(ts(fac_w[:], fac_v[:], phase[:, 1:2], ROUND, ALU.add, ALU.add))
            stt(fac_w[:], fac_w[:], ROUND, fac_v[:], ALU.subtract, ALU.subtract).then_inc(fac_in, 1)
            dve.wait_ge(fac_out, 2)
            link(tt(fac_u[:], fac_u[:], fac_t[:], ALU.mult))
            link(tt(fac_u[:], fac_u[:], across(2), ALU.mult))
            dve.wait_ge(fac_out, 3)
            link(tt(fac_w[:], fac_w[:], fac_t[:], ALU.mult))
            link(tt(fac_w[:], fac_w[:], across(3), ALU.mult))
            link(tt(fac_u[:], fac_u[:], fac_w[:], ALU.add))
            link(tt(fac_v[:], across(1), steps_of(1), ALU.mult))
            link(ts(fac_w[:], fac_v[:], phase[:, 2:3], ROUND, ALU.add, ALU.add))
            stt(fac_w[:], fac_w[:], ROUND, fac_v[:], ALU.subtract, ALU.subtract).then_inc(fac_in, 1)
            tt(fac_t[:], across(0), steps_of(1), ALU.mult).then_inc(fac_in, 1)
            dve.wait_ge(fac_out, 5)
            tt(fac_v[:], fac_w[:], fac_t[:], ALU.mult).then_inc(factors, 1)

            for i in range(K8):
                j = J_W3 + i
                dve.wait_ge(job_done, j + 1)
                tt(p3[:, i, :], ps[j % 4][:], diag[:, K8 - 1 - i:K8 - 1 - i + T], ALU.add).then_inc(job_free, 1)

            highs = [0]

            def low(j, to, of, high):
                highs[0] += 1
                dve.wait_ge(job_hi, highs[0])
                tt(to, of, f(high), ALU.subtract).then_inc(job_free, 1)

            for i in range(K8):
                low(J_LA + i, lora_in[:, 1, i, 0:AR], ps[(J_LA + i) % 4][:, 0:AR], lora_in[:, 0, i, 0:AR])
            for i in range(half_t):
                low(J_D0 + i, dense0[:, 1, i, :], ps[(J_D0 + i) % 4][:], dense0[:, 0, i, :])
            for i in range(2):
                j = J_K + i
                dve.wait_ge(job_done, j + 1)
                nc.vector.tensor_copy(kern[:, i * C // 2:(i + 1) * C // 2, :],
                                      ps[j % 4][0:G, :].rearrange("q (h r) -> q h r", r=G)).then_inc(job_free, 1)
            dve.wait_ge(job_free, J_K + 2)
            link(ts(dcol[:], dcol[:], 1.0, last[:], ALU.add, ALU.mult))
            tt(kern[:, :, G - 1], kern[:, :, G - 1], dcol[:], ALU.add).then_inc(kern_ready, 1)
            for i in range(half_t):
                low(J_D1 + i, dense1[:, 1, i, :], ps[(J_D1 + i) % 4][:], dense1[:, 0, i, :])
            for i in range(K8):
                low(J_A3 + i, lora_in[:, 1, i, AR:AR + LR], ps[(J_A3 + i) % 4][:, 0:LR], lora_in[:, 0, i, AR:AR + LR])
            dve.wait_ge(job_done, J_C + 1)
            nc.vector.tensor_copy(ct[:, 0, :], ps[J_C % 4][:, 0:AR + 1]).then_inc(job_free, 1)
            dve.wait_ge(job_done, J_C + 2)
            nc.vector.tensor_copy(ct[0:R3, 1, :], ps[(J_C + 1) % 4][0:R3, 0:AR + 1]).then_inc(job_free, 1)
            for m in range(AR // P + 1):
                j = J_B2 + m
                dve.wait_ge(job_done, j + 1)
                if m < AR // P:
                    nc.vector.tensor_copy(b2p[:, m, :], ps[j % 4][:]).then_inc(job_free, 1)
                else:
                    nc.vector.tensor_copy(b2p_bias[:], ps[j % 4][0:1, :]).then_inc(job_free, 1)
            dve.wait_ge(job_done, J_B3 + 1)
            ts(b3t[:], ps[J_B3 % 4][:], 0.5, None, ALU.mult).then_inc(b3_ready, 1)
            dve.wait_ge(b3_ready, 2)
            tt(b3s[:, 1], b3t[:], f(b3s[:, 0]), ALU.subtract).then_inc(job_free, 1)
            for s, (l, m) in enumerate(FOLDS):
                j = J_F + s
                dve.wait_ge(job_done, j + 1)
                if s >= 2:
                    dve.wait_ge(fold_lo, s - 1)
                if m < AR // P:
                    tt(fold[s % 2][:], ps[j % 4][:], b2p[:, m, :], ALU.add).then_inc(fold_sum, 1)
                else:
                    tt(fold[s % 2][0:1, :], ps[j % 4][0:1, :], b2p_bias[:], ALU.add).then_inc(fold_sum, 1)

            def transposed_low(k, u):
                dve.wait_ge(ut_hi, 4 * k + u + 1)
                tt(ut[u % 2][:, 1], ps[u % 2][:].rearrange("p (i b) -> p i b", i=K8), f(ut[u % 2][:, 0]),
                   ALU.subtract).then_inc(ut_lo, 1)

            def masked(k, u):
                dve.wait_ge(conv_done, 4 * k + u + 1)
                dve.sem_inc(mask_begun, 1)
                dve.wait_ge(chain, mask_made)
                nc.vector.copy_predicated(xt[u][:], mask[:], ps[2 + u % 2][:]).then_inc(x1_ready, 1)

            def channel(k, u, ahead=True):
                if ahead:
                    transposed_low(k + (u + 1) // 4, (u + 1) % 4)
                masked(k, u)

            transposed_low(0, 0)
            with dve.Fori(0, GROUPS - 1) as k:
                for u in range(4):
                    channel(k, u)
            for u in range(4):
                channel(GROUPS - 1, u, ahead=u < 3)

        @block.tensor
        def _(pe):
            mm = nc.tensor.matmul

            def job(j):
                if j >= 4:
                    wait_free(j - 3)
                return ps[j % 4]

            def wait_free(n):
                pe.wait_ge(job_free, min(n, J_F))
                if n > J_F:
                    pe.wait_ge(fold_sum, n - J_F)

            def over_chunks(out_ap, lhs, rhs):
                for i in range(K8):
                    ins = mm(out_ap, lhs(i), rhs(i), start=i == 0, stop=i == K8 - 1)
                return ins

            pe.wait_ge(base_ready, 1)
            pe.wait_ge(consts, 2)
            t = job(J_PAR)
            for q in range(4):
                ins = nc.tensor.transpose(t[:, q * C:(q + 1) * C], par[:, q * 2 * N:(q + 1) * 2 * N], ident[0:C, 0:C])
            ins.then_inc(job_done, 1)

            pe.wait_ge(in_w3, 16)
            for i in range(K8):
                t = job(J_W3 + i)
                for c in range(K8):
                    ins = nc.tensor.transpose(t[:, c * P:(c + 1) * P], w3_raw[:, c, i:i + K8 * (P - 1) + 1:K8], ident[:])
                ins.then_inc(job_done, 1)
            pe.wait_ge(in_la, 16)
            for i in range(K8):
                t = job(J_LA + i)
                for c in range(AR // P):
                    ins = nc.tensor.transpose(t[:, c * P:(c + 1) * P], lora_a_raw[:, c, i * P:(i + 1) * P], ident[:])
                ins.then_inc(job_done, 1)

            def dense_job(j, i):
                t = job(j)
                for half in range(2):
                    cols = slice(half * HB, (half + 1) * HB)
                    ins = over_chunks(t[:, cols], lambda c: p2[:, c, i * P:(i + 1) * P], lambda c: p3[:, c, cols])
                ins.then_inc(job_done, 1)

            pe.wait_ge(p2_ready, 1)
            pe.wait_ge(job_free, J_W3 + K8)
            for i in range(half_t):
                dense_job(J_D0 + i, i)
            pe.wait_ge(factors, 1)
            for q in range(2):
                t = job(J_K + q)
                for h in range(C // 2):
                    c = q * C // 2 + h
                    ins = mm(t[0:G, h * G:(h + 1) * G], fac_u[:, c, :], fac_v[:, c, :], start=True, stop=True)
                ins.then_inc(job_done, 1)
            for i in range(half_t):
                dense_job(J_D1 + i, half_t + i)
            pe.wait_ge(in_lb, 16 * (2 * K8 + 5))
            for i in range(K8):
                t = job(J_A3 + i)
                over_chunks(t[:, 0:LR], lambda c: p2[:, c, i * P:(i + 1) * P], lambda c: a3raw[:, c, :]).then_inc(job_done, 1)
            for q, cols in enumerate((slice(0, P), slice(P, LR))):
                t = job(J_C + q)
                rows = cols.stop - cols.start
                over_chunks(t[0:rows, 0:AR], lambda c: a3raw[:, c, cols], lambda c: b2raw[:, c, :])
                over_chunks(t[0:rows, AR:AR + 1], lambda c: a3raw[:, c, cols], lambda c: bias_col[:, c:c + 1]).then_inc(job_done, 1)
            for m in range(AR // P + 1):
                t = job(J_B2 + m)
                for half in range(2):
                    cols = slice(half * HB, (half + 1) * HB)
                    if m < AR // P:
                        ins = over_chunks(t[:, cols], lambda c: b2raw[:, c, m * P:(m + 1) * P], lambda c: p3[:, c, cols])
                    else:
                        ins = over_chunks(t[0:1, cols], lambda c: bias_col[:, c:c + 1], lambda c: p3[:, c, cols])
                ins.then_inc(job_done, 1)
            t = job(J_B3)
            for c in range(K8):
                ins = nc.tensor.transpose(t[:, c * P:(c + 1) * P], b3rep[:, c, :, :].rearrange("p a r -> p (a r)"), ident[:])
            ins.then_inc(job_done, 1)
            pe.wait_ge(b3_ready, 1)
            for s, (l, m) in enumerate(FOLDS):
                t = job(J_F + s)
                rows = slice(R3 * (l % 4), R3 * (l % 4) + R3)
                width = P if m < AR // P else 1
                for half in range(2):
                    cols = slice(half * HB, (half + 1) * HB)
                    ins = mm(t[0:width, cols], ct[rows, l // 4, m * P:m * P + width], b3t[rows, cols], start=True, stop=True)
                ins.then_inc(job_done, 1)

            def transpose_x(k, u):
                h = 4 * k + u
                pe.wait_ge(x_in[u], 16 * k + 16)
                ready(pe, ut_lo, h - 1)
                for i in range(K8):
                    ins = nc.tensor.transpose(ps[u % 2][:, i * P:(i + 1) * P], xt[u][:, i * P:(i + 1) * P], ident[:])
                ins.then_inc(ut_ps, 1)

            def convolve(k, u):
                h = 4 * k + u
                pe.wait_ge(toep_lo, h + 1)
                pe.wait_ge(ut_lo, h + 1)
                ready(pe, x1_ready, h - 1)
                y, xs, tp = ps[2 + u % 2], ut[u % 2], toep[u % 2]
                for i in range(K8):
                    for a in range(2):
                        for b in range(2 - a):
                            for bank in range(2):
                                lo, hi = max(i * P, bank * HB), (bank + 1) * HB
                                if lo < hi:
                                    ins = mm(y[:, lo:hi], xs[:, a, i, :], tp[:, b, lo - i * P:hi - i * P],
                                             start=i == 0 and a == 0 and b == 0,
                                             stop=a == 1 and i == (bank + 1) * half_t - 1)
                ins.then_inc(conv_done, 1)

            wait_free(JOBS)
            transpose_x(0, 0)

            def channel(k, u, ahead=True):
                if ahead:
                    transpose_x(k + (u + 1) // 4, (u + 1) % 4)
                convolve(k, u)

            for u in range(4):
                channel(0, u)
            with pe.Fori(1, GROUPS - 1) as k:
                for u in range(4):
                    channel(k, u)
            for u in range(4):
                channel(GROUPS - 1, u, ahead=u < 3)


    x1_landed = [sem(f"x1_landed{i}") for i in range(2)]
    stack_landed = [sem(f"stack_landed{i}") for i in range(2)]
    y_stored = [sem(f"y_stored{i}") for i in range(2)]
    x1_hi, x1_lo = sem("x1_hi"), sem("x1_lo")
    gathered_m, gathered_a = sem("gathered_m"), sem("gathered_a")
    x2_ps, x2_hi, x2_lo = sem("x2_ps"), sem("x2_hi"), sem("x2_lo")
    h_ps, h_sum, h_hi, h_lo = sem("h_ps"), sem("h_sum"), sem("h_hi"), sem("h_lo")
    y_ps, y_left, y_right = sem("y_ps"), sem("y_left"), sem("y_right")
    fixed, gfixed = sem("fixed"), sem("gfixed")
    PAIRS = TILES // 2
    x1_rows = x1_d.rearrange("(n b) c t -> n (b c) t", b=2)
    out_rows = out.rearrange("(n b) c t -> n (b c) t", b=2)

    def over_tiles(eng, body):
        for v in range(2):
            body(0, v)
        with eng.Fori(1, PAIRS - 1) as k:
            for v in range(2):
                body(k, v)
        for v in range(2):
            body(PAIRS - 1, v)

    def exists(k, v):
        return not isinstance(k, int) or 2 * k + v < TILES

    with nc.Block() as block:
        @block.sync
        def _(sp):
            def load_x1(k, v):
                k, v = k + v // 2, v % 2
                n = 2 * k + v
                ready(sp, x1_lo, n - 1)
                sp.dma_start(x1_in[v][:], x1_rows[bass.ds(n, 1)].squeeze(0)).then_inc(x1_landed[v], 16)

            def load_stack(k, v):
                k, v = k + v // 2, v % 2
                n = 2 * k + v
                ready(sp, y_ps, n - 1)
                for b in range(2):
                    a = sp.value_load(index[0:1, bass.ds(2 * n + b + B, 1)], min_val=0, max_val=A2N - 1)
                    l = sp.value_load(index[0:1, bass.ds(2 * n + b + 2 * B, 1)], min_val=0, max_val=L3N - 1)
                    sp.dma_start(f(stack[v][b * R2:(b + 1) * R2]), b2_d[bass.ds(l * A2N + a, 1)].squeeze(0)).then_inc(stack_landed[v], 16)
                    sp.dma_start(f(stack[v][KR + b:KR + b + 1]), row_d[bass.ds(l, 1)].squeeze(0)).then_inc(stack_landed[v], 16)

            def tile(k, v):
                if exists(k, v + 2):
                    load_x1(k, v + 2)
                n = 2 * k + v
                sp.wait_ge(y_left, n + 1)
                sp.wait_ge(y_right, n + 1)
                sp.dma_start(out_rows[bass.ds(n, 1)].squeeze(0), y_out[v][:]).then_inc(y_stored[v], 16)
                if exists(k, v + 2):
                    load_stack(k, v + 2)

            for v in range(2):
                load_x1(0, v)
                load_stack(0, v)
            over_tiles(sp, tile)
            for v in range(2):
                sp.wait_ge(y_stored[v], 16 * PAIRS)

        @block.gpsimd
        def _(pool):
            for v in range(2):
                nc.gpsimd.memset(f(m_gath[v][:]), 0.0).then_inc(gfixed, 1)
            pool.wait_ge(gfixed, 2)

            def gather(k, v):
                k, v = k + v // 2, v % 2
                n = 2 * k + v
                ready(pool, x2_ps, n - 1)
                pool.wait_ge(x1_lo, n + 1)
                for b in range(2):
                    s = pool.value_load(index[0:1, bass.ds(2 * n + b, 1)], min_val=0, max_val=S1 - 1)
                    rows = slice(b * C, (b + 1) * C)
                    ins = nc.gpsimd.tensor_copy(m_gath[v][rows, :, b * C:(b + 1) * C],
                                                f(mix[rows, :, bass.ds(s, 1), :].squeeze(2)))
                ins.then_inc(gathered_m, 1)
                pool.wait_ge(gathered_m, n + 1)
                ready(pool, h_ps, n - 1)
                to = a_gath[v][:].rearrange("p h i m -> p (h i) m")
                of = f(lora_in[:].rearrange("p h i m -> p (h i) m"))
                for b in range(2):
                    a = pool.value_load(index[0:1, bass.ds(2 * n + b + B, 1)], min_val=0, max_val=A2N - 1)
                    l = pool.value_load(index[0:1, bass.ds(2 * n + b + 2 * B, 1)], min_val=0, max_val=L3N - 1)
                    nc.gpsimd.tensor_copy(to[:, :, b * R2:(b + 1) * R2], of[:, :, bass.ds(a * R2, R2)])
                    c = 2 * R2 + b * R3
                    ins = nc.gpsimd.tensor_copy(to[:, :, c:c + R3], of[:, :, bass.ds(l * R3 + AR, R3)])
                ins.then_inc(gathered_a, 1)

            def split_low(k, v):
                k, v = k + v // 2, v % 2
                pool.wait_ge(x1_hi, 2 * k + v + 1)
                nc.gpsimd.tensor_tensor(x1s[v][:, 1], x1_in[v][:], f(x1s[v][:, 0]), ALU.subtract).then_inc(x1_lo, 1)

            for v in range(2):
                split_low(0, v)
                gather(0, v)

            def tile(k, v):
                if exists(k, v + 2):
                    split_low(k, v + 2)
                    gather(k, v + 2)

            over_tiles(pool, tile)

        @block.scalar
        def _(act):
            def split_high(k, v):
                k, v = k + v // 2, v % 2
                n = 2 * k + v
                act.wait_ge(x1_landed[v], 16 * k + 16)
                ready(act, x2_ps, n - 1)
                nc.scalar.activation(x1s[v][:, 0], x1_in[v][:], ACT.Copy).then_inc(x1_hi, 1)

            def x2_high(k, v):
                k, v = k + v // 2, v % 2
                n = 2 * k + v
                act.wait_ge(x2_ps, n + 1)
                ready(act, y_ps, n - 1)
                nc.scalar.activation(x2t[v][:, 0], ps[0][:].rearrange("p (i m) -> p i m", i=K8), ACT.Copy).then_inc(x2_hi, 1)

            def tile(k, v):
                if exists(k, v + 1):
                    x2_high(k, v + 1)
                if exists(k, v + 2):
                    split_high(k, v + 2)
                n = 2 * k + v
                act.wait_ge(y_ps, n + 1)
                if not isinstance(k, int) or k > 0:
                    act.wait_ge(y_stored[v], 16 * k)
                nc.scalar.activation(y_out[v][:, 0:HB], ps[2 + v][:, 0:HB], ACT.Copy).then_inc(y_left, 1)

            for v in range(2):
                split_high(0, v)
            x2_high(0, 0)
            over_tiles(act, tile)

        @block.vector
        def _(dve):
            tt = nc.vector.tensor_tensor
            made = [0]

            def fix(ins):
                made[0] += 1
                ins.then_inc(fixed, 1)
                dve.wait_ge(fixed, made[0])

            fix(nc.vector.memset(hmask[:], 0.0))
            fix(nc.vector.memset(hmask[0:R2, 0:C], 1.0))
            fix(nc.vector.memset(hmask[2 * R2:2 * R2 + R3, 0:C], 1.0))
            fix(nc.vector.memset(hmask[2 * R2 + R3:KR, C:P], 1.0))
            fix(nc.vector.tensor_reduce(hm[0][0:2 * R2, 0:1], ident[0:2 * R2, R2:2 * R2], mybir.AxisListType.X, ALU.add))
            fix(nc.vector.tensor_copy(hmask[0:2 * R2, C:P], hm[0][0:2 * R2, 0:1].to_broadcast([2 * R2, C])))
            for b in range(2):
                fix(nc.vector.tensor_copy(hmask[KR:KR + 2, b * C:(b + 1) * C], ident[KR:KR + 2, KR + b:KR + b + 1].to_broadcast([2, C])))
            for v in range(2):
                fix(nc.vector.tensor_copy(hs[v][KR:KR + 2, 0], hmask[KR:KR + 2, :]))
                fix(nc.vector.memset(f(hs[v][KR:KR + 2, 1]), 0.0))
                for q in range(2):
                    rows = slice(2 * R2 + q * R3, 2 * R2 + (q + 1) * R3)
                    fix(nc.vector.tensor_copy(stack[v][rows], f(b3s[rows])))

            def x2_low(k, v):
                k, v = k + v // 2, v % 2
                dve.wait_ge(x2_hi, 2 * k + v + 1)
                tt(x2t[v][:, 1], ps[0][:].rearrange("p (i m) -> p i m", i=K8), f(x2t[v][:, 0]), ALU.subtract).then_inc(x2_lo, 1)

            def low_rank(k, v):
                n = 2 * k + v
                dve.wait_ge(h_ps, n + 1)
                ready(dve, y_ps, n - 1)
                tt(hm[v][:], ps[1][0:KR, v * HB:v * HB + P], hmask[0:KR, :], ALU.mult).then_inc(h_sum, 1)
                dve.wait_ge(h_sum, n + 1)
                nc.vector.tensor_copy(hs[v][0:KR, 0], hm[v][:]).then_inc(h_hi, 1)
                dve.wait_ge(h_hi, n + 1)
                tt(hs[v][0:KR, 1], hm[v][:], f(hs[v][0:KR, 0]), ALU.subtract).then_inc(h_lo, 1)

            def tile(k, v):
                if exists(k, v + 1):
                    x2_low(k, v + 1)
                low_rank(k, v)
                n = 2 * k + v
                dve.wait_ge(y_ps, n + 1)
                if not isinstance(k, int) or k > 0:
                    dve.wait_ge(y_stored[v], 16 * k)
                nc.vector.tensor_copy(y_out[v][:, HB:T], ps[2 + v][:, HB:T]).then_inc(y_right, 1)

            x2_low(0, 0)
            over_tiles(dve, tile)

        @block.tensor
        def _(pe):
            mm = nc.tensor.matmul
            PASSES = ((0, 0), (0, 1), (1, 0))

            def mixing(k, v):
                k, v = k + v // 2, v % 2
                n = 2 * k + v
                pe.wait_ge(x1_lo, n + 1)
                pe.wait_ge(gathered_m, n + 1)
                ready(pe, x2_lo, n)
                for i in range(K8):
                    for a, b in PASSES:
                        ins = mm(ps[0][:, i * P:(i + 1) * P], x1s[v][:, a, i * P:(i + 1) * P], m_gath[v][:, b, :],
                                 start=a == b == 0, stop=a == 1)
                ins.then_inc(x2_ps, 1)

            def low_rank(k, v):
                n = 2 * k + v
                pe.wait_ge(x2_lo, n + 1)
                pe.wait_ge(gathered_a, n + 1)
                ready(pe, h_lo, n - 1)
                for i in range(K8):
                    for a, b in PASSES:
                        ins = mm(ps[1][0:KR, v * HB:v * HB + P], a_gath[v][:, a, i, :], x2t[v][:, b, i, :],
                                 start=i == 0 and a == b == 0, stop=i == K8 - 1 and a == 1)
                ins.then_inc(h_ps, 1)

            def dense(k, v):
                n = 2 * k + v
                ready(pe, y_left, n - 1)
                ready(pe, y_right, n - 1)
                y = ps[2 + v]
                for i in range(K8):
                    w = (dense0, dense1)[i // half_t]
                    for a in range(2):
                        for b in range(2 - a):
                            for half in range(2):
                                cols = slice(half * HB, (half + 1) * HB)
                                mm(y[:, cols], x2t[v][:, a, i, :], w[:, b, i % half_t, cols],
                                   start=i == 0 and a == b == 0, stop=False)
                pe.wait_ge(h_lo, n + 1)
                pe.wait_ge(stack_landed[v], 64 * k + 64)
                if isinstance(k, int) and k == 0:
                    pe.wait_ge(fixed, FIXED)
                for a in range(2):
                    for b in range(2 - a):
                        for half in range(2):
                            cols = slice(half * HB, (half + 1) * HB)
                            ins = mm(y[:, cols], hs[v][:, a, :], stack[v][:, b, cols], start=False, stop=a == 1)
                ins.then_inc(y_ps, 1)

            def tile(k, v):
                if exists(k, v + 1):
                    mixing(k, v + 1)
                low_rank(k, v)
                dense(k, v)

            mixing(0, 0)
            over_tiles(pe, tile)


_INS = ["x", "itok_B_8_3872", "itok_B_0_15", "itok_B_6_15", "itok_B_0_2", "L0_cond_log_dt", "L0_cond_C",
        "L0_cond_log_A_real", "L0_cond_A_imag", "L0_cond_D", "L1_cond_weights", "L2_cond_base_weight",
        "L2_cond_base_bias", "L2_cond_lora_A_w", "L2_cond_lora_B_w", "L3_cond_W", "L3_cond_lora_A", "L3_cond_lora_B_w"]


def kernel(**inputs):
    import numpy as np
    from concourse import bacc
    from concourse.bass_utils import run_bass_kernel_spmd

    nc = bacc.Bacc("TRN2", target_bir_lowering=False, num_devices=1, dynamic_dma_scratch_size=1024)
    arrays, args = {}, []
    for name in _INS:
        a = np.ascontiguousarray(inputs[name])
        arrays[f"in_{name}"] = a
        args.append(nc.dram_tensor(f"in_{name}", a.shape, mybir.dt.from_np(a.dtype), kind="ExternalInput").ap())
    args.append(nc.dram_tensor("out_0", (B, C, T), F32, kind="ExternalOutput").ap())
    program(nc, *args)
    r = run_bass_kernel_spmd(nc, [arrays], core_ids=[0])
    return r.results[0]["out_0"]
```

```python
import math

import concourse.bass as bass
from concourse import mybir

F32, F32R = mybir.dt.float32, mybir.dt.float32r
I32, U8 = mybir.dt.int32, mybir.dt.uint8
ALU = mybir.AluOpType
ACT = mybir.ActivationFunctionType

B, C, T = 128, 64, 1024
N = 64
P = 128
K8 = T // P
S1 = 16
A2N, R2 = 32, 16
L3N, R3 = 5, 32
AR, LR = A2N * R2, L3N * R3
G = 32
HB = T // 2
TILES = B // 2
KR = 2 * R2 + 2 * R3
KC = 2 * R2 + 2
ROUND = 1.5 * 2.0 ** 23
TWO_PI = 6.283184
LOG2E = 1.4426950408889634
LN2_HI, LN2_LO = 0.693145751953125, 1.4286068203094172e-06
LAYOUT_END = 229368


def program(nc, x, steps, cond, adapter, labeler, log_dt, ssm_c, log_a_real, a_imag, ssm_d,
            mix_w, w2, bias2, lora2_a, lora2_b, w3, lora3_a, lora3_b, out):
    base = (nc.sbuf_base + 63) // 64 * 64

    def at(name, shape, dtype, offset):
        size = math.prod(shape[1:]) * mybir.dt.size(dtype)
        assert base + offset + size <= LAYOUT_END, (name, base + offset + size)
        return nc.alloc_sbuf_tensor_at(name, shape, dtype, offset=base + offset), (offset + size + 31) // 32 * 32

    half_t = K8 // 2
    dense0, o_dense1 = at("dense0", [P, 2, half_t, T], F32R, 0)
    dense1, o_lora2 = at("dense1", [P, 2, half_t, T], F32R, o_dense1)
    lora2_in, o = at("lora2_in", [P, K8, AR], F32, o_lora2)
    lora3_in, o = at("lora3_in", [P, K8, LR], F32, o)
    mix, o = at("mix", [P, S1, C], F32, o)
    b3t, o = at("b3t", [P, T], F32, o)
    bias_row, o = at("bias_row", [1, T], F32, o)
    ident, o = at("ident", [P, P], F32, o)
    index, o = at("index", [1, 3 * B], I32, o)
    mask, o_phase = at("mask", [P, T], U8, o)

    w3_raw, o = at("w3_raw", [P, K8, T], F32, 0)
    assert o <= o_dense1
    fac_u, o = at("fac_u", [P, C, G], F32, o_dense1)
    fac_v, o = at("fac_v", [P, C, G], F32, o)
    fac_w, o_fac_t = at("fac_w", [P, C, G], F32, o)
    fac_t, o = at("fac_t", [P, C, G], F32, o_fac_t)
    kern, _ = at("kern", [G, C, G], F32, o_fac_t)
    ramp, _ = at("ramp", [P, T], F32, o_fac_t)
    assert o <= o_lora2
    waste, _ = at("waste", [P, T], F32, o_lora2 + 4 * K8 * AR)
    b2raw, o = at("b2raw", [P, K8, AR], F32, o_lora2)
    p2, o_p3 = at("p2", [P, K8, T], F32, o_phase)
    p3, o_st = at("p3", [P, 2, K8, T], F32R, o_p3)
    staged, o = [], o_st
    for i in range(2):
        t, o = at(f"staged{i}", [P, 2, K8, P], F32R, o)
        staged.append(t)
    o_staged_end = o
    a3raw, o = at("a3raw", [P, K8, LR], F32, o)
    b3rep, o = at("b3rep", [P, K8, 4, R3], F32, o)
    part, o = at("part", [P, 4, C], F32, o)
    grid, o = at("grid", [P, 2, G], F32, o)
    phase, o = at("phase", [P, 6], F32, o)
    last, o = at("last", [G, 1], F32, o)
    dcol, o = at("dcol", [G, C], F32, o)
    bias_col, o = at("bias_col", [P, K8], F32, o)
    bias_p3, o = at("bias_p3", [P, K8], F32, o)
    lora_a_raw, o = at("lora_a_raw", [P, AR // P, T], F32, o_phase)
    b2_out, o = at("b2_out", [P, 2, T], F32R, o)
    c_out = []
    for i in range(AR // P + 1):
        t, o = at(f"c_out{i}", [P, LR], F32, o)
        c_out.append(t)
    assert o <= o_p3

    o = o_st
    def nat(name, cols, dtype=F32, parts=C):
        nonlocal o
        t, o = at(name, [parts, cols], dtype, o)
        return t
    logs, exps = nat("logs", N + 1), nat("exps", N + 1)
    e_k, e_f, e_q, e_2k = (nat(f"e_{n}", N + 1) for n in "kfqs")
    e_i = nat("e_i", N + 1, I32)
    aim, cri = nat("aim", N), nat("cri", 2 * N)
    decay, angle, em1, turns, frac, sin1, sinh, cosm1, zr, zi, den, nr, ni, tmp, tmp2 = (
        nat(f"n_{n}", N) for n in range(15))
    par = nat("par", 4 * 2 * N)
    lens_i, lens = nat("lens_i", 1, I32, P), nat("lens", 1, parts=P)
    bias8 = nat("bias8", P, parts=K8)
    zero = nat("zero", P)
    assert o <= o_staged_end, o - o_staged_end
    ut, toep, toep_raw, xt = [], [], [], []
    o = o_p3
    for names, two, shape, dtype in (("ut", ut, [P, 2, K8, P], F32R), ("toep", toep, [P, 2, T], F32R),
                                     ("toep_raw", toep_raw, [P, T], F32), ("xt", xt, [P, T], F32),
                                     ("xt_", xt, [P, T], F32)):
        for i in range(2):
            t, o = at(f"{names}{i}", shape, dtype, o)
            two.append(t)
    assert o <= o_st

    o = o_phase
    def pair(name, shape, dtype=F32):
        nonlocal o
        two = []
        for i in range(2):
            t, o = at(f"{name}{i}", shape, dtype, o)
            two.append(t)
        return two
    x1_in = pair("x1_in", [P, T])
    x2f = pair("x2f", [P, K8, P])
    x2t = pair("x2t", [P, 2, K8, P], F32R)
    y_out = pair("y_out", [P, T])
    a_gath = pair("a_gath", [P, K8, KR])
    m_gath = pair("m_gath", [P, P])
    c_gath = pair("c_gath", [KC, KR])
    stack = pair("stack", [KR + 1, 2, T], F32R)
    hs = pair("hs", [KR + 1, 2, P], F32R)
    hc = pair("hc", [KC, P])
    hm = pair("hm", [KR, P])
    hmask, o = at("hmask", [KR, P], F32, o)

    ps = [nc.alloc_psum_tensor(f"ps{i}", [P, T], F32) for i in range(4)]
    kern_d = nc.dram_tensor("kern_d", [C, T + P], F32).ap()
    x1_d = nc.dram_tensor("x1_d", [B, C, T], F32).ap()
    b2_d = nc.dram_tensor("b2_d", [A2N, R2, 2, T], F32).ap()
    c_d = nc.dram_tensor("c_d", [AR + 1, LR], F32).ap()

    def f(ap):
        return ap.bitcast(F32)

    J_PAR = 0
    J_W3 = J_PAR + 1
    J_D0 = J_W3 + K8
    J_K = J_D0 + half_t
    J_D1 = J_K + 2
    J_A3 = J_D1 + half_t
    J_C = J_A3 + K8
    J_B2 = J_C + AR // P + 1
    J_ROW = J_B2 + AR // P
    J_LA = J_ROW + 2
    JOBS = J_LA + K8
    SMALL = 10
    CONSTS, FIXED = 7 + 12 + 1, 21

    sem = nc.alloc_semaphore
    in_small, in_bias, in_w3, in_la, in_w2, in_b2, in_a3, in_b3, in_mix = (
        sem(f"in_{n}") for n in ("small", "bias", "w3", "la", "w2", "b2", "a3", "b3", "mix"))
    consts = sem("consts")
    chain = sem("chain")
    pchain = sem("pchain")
    base_ready = sem("base_ready")
    trig_in, trig_out = sem("trig_in"), sem("trig_out")
    part_ready = sem("part_ready")
    fac_turns, fac_decay = sem("fac_turns"), sem("fac_decay")
    fac_arg, fac_sin, fac_exp = sem("fac_arg"), sem("fac_sin"), sem("fac_exp")
    factors = sem("factors")
    w3_ready, p2_ready, mix_ready = sem("w3_ready"), sem("p2_ready"), sem("mix_ready")
    job_done, job_hi = sem("job_done"), sem("job_hi")
    job_free = sem("job_free")
    staged_hi, staged_lo = sem("staged_hi"), sem("staged_lo")
    kern_ready, kern_stored = sem("kern_ready"), sem("kern_stored")
    bias_ready = sem("bias_ready")
    b2_hi, b2_stored = sem("b2_hi"), sem("b2_stored")
    c_stored = sem("c_stored")

    def ready(eng, semaphore, value):
        if not isinstance(value, int) or value > 0:
            eng.wait_ge(semaphore, value)

    x_in = [sem(f"x_in{i}") for i in range(4)]
    x1_stored = [sem(f"x1_stored{i}") for i in range(4)]
    toep_in = [sem(f"toep_in{i}") for i in range(2)]
    toep_hi, toep_lo = sem("toep_hi"), sem("toep_lo")
    ut_ps, ut_hi, ut_lo = sem("ut_ps"), sem("ut_hi"), sem("ut_lo")
    conv_done, x1_ready = sem("conv_done"), sem("x1_ready")
    mask_begun = sem("mask_begun")
    GROUPS = C // 4

    def over_channels(eng, body):
        for u in range(4):
            body(0, u)
        with eng.Fori(1, GROUPS) as k:
            for u in range(4):
                body(k, u)

    toep_view = bass.AP(tensor=kern_d.tensor, offset=0, ap=[[T + P, C], [1, P], [1, T]])
    b2_rows = b2_d.rearrange("a r h t -> (a r) h t")
    STAGES = [p2[:, :, i * P:(i + 1) * P] for i in range(K8)] + [b2raw[:, :, i * P:(i + 1) * P] for i in range(AR // P)]
    STAGE_JOBS = list(range(J_D0, J_D0 + half_t)) + list(range(J_D1, J_D1 + half_t)) + list(range(J_B2, J_B2 + AR // P))

    with nc.Block() as block:
        @block.sync
        def _(sp):
            for to, of in ((logs[:, 0:N], log_a_real), (logs[:, N:N + 1], log_dt.unsqueeze(1)),
                           (aim[:], a_imag), (cri[:], ssm_c.rearrange("h n c -> h (n c)")),
                           (dcol[:], ssm_d.unsqueeze(0).to_broadcast([G, C])),
                           (lens_i[:], steps.unsqueeze(1)),
                           (index[:, 0:B], cond.unsqueeze(0)), (index[:, B:2 * B], adapter.unsqueeze(0)),
                           (index[:, 2 * B:3 * B], labeler.unsqueeze(0)),
                           (bias8[:], bias2.rearrange("(c p) -> c p", p=P))):
                sp.dma_start(to, of).then_inc(in_small, 16)
            sp.dma_start(w3_raw[:], w3.rearrange("(c p) d -> p c d", p=P)).then_inc(in_w3, 16)
            sp.dma_start(b3t[:], bias2.unsqueeze(0).to_broadcast([P, T])).then_inc(in_bias, 16)
            sp.dma_start(p2[:], w2.rearrange("(c p) t -> p c t", p=P)).then_inc(in_w2, 16)
            for half in range(2):
                sp.dma_start(mix[C * half:C * half + C], mix_w.rearrange("s c d -> c s d")).then_inc(in_mix, 16)
            for c in range(K8):
                sp.dma_start(a3raw[:, c, :].rearrange("p (l r) -> p l r", r=R3),
                             lora3_a.rearrange("l (c p) r -> c p l r", p=P)[c]).then_inc(in_a3, 16)
            for c in range(K8):
                sp.dma_start(b2raw[:, c, :].rearrange("p (a r) -> p a r", r=R2),
                             lora2_b.rearrange("a (c p) r -> c p a r", p=P)[c]).then_inc(in_b2, 16)
            for copy in range(4):
                sp.dma_start(b3rep[:, :, copy, :], lora3_b.rearrange("(c p) r -> p c r", p=P)).then_inc(in_b3, 16)

            sp.wait_ge(consts, 7)
            sp.dma_start(kern_d[:, T:T + P], zero[:]).then_inc(kern_stored, 16)
            sp.wait_ge(kern_ready, 1)
            sp.dma_start(kern_d[:, 0:T].rearrange("h (q r) -> q h r", q=G), kern[:]).then_inc(kern_stored, 16)

            sp.wait_ge(job_done, J_A3 + K8)
            sp.dma_start(lora_a_raw[:], lora2_a.rearrange("(c a) r t -> (a r) c t", c=AR // P)).then_inc(in_la, 16)
            for m in range(AR // P + 1):
                sp.wait_ge(job_free, J_C + m)
                rows = P if m < AR // P else 1
                sp.dma_start(c_d[m * P:m * P + rows], c_out[m][0:rows]).then_inc(c_stored, 16)
            for m in range(AR // P):
                sp.wait_ge(job_free, J_B2 + m)
                sp.dma_start(b2_rows[m * P:(m + 1) * P], f(b2_out[:])).then_inc(b2_stored, 16)

            def load_x(k, u):
                if not isinstance(k, int) or k > 0:
                    sp.wait_ge(x1_stored[u], 16 * k)
                sp.dma_start(xt[u][:], x[:, bass.ds(4 * k + u, 1), :].squeeze(1)).then_inc(x_in[u], 16)

            def load_toep(k, u):
                h = 4 * k + u
                ready(sp, toep_hi, h - 1)
                ready(sp, toep_lo, h - 1)
                sp.dma_start(toep_raw[u % 2][:], toep_view[bass.ds(h, 1), :, :].squeeze(0)).then_inc(toep_in[u % 2], 16)

            def store_x1(k, u):
                sp.wait_ge(x1_ready, 4 * k + u + 1)
                sp.dma_start(x1_d[:, bass.ds(4 * k + u, 1), :].squeeze(1), xt[u][:]).then_inc(x1_stored[u], 16)

            sp.wait_ge(kern_stored, 32)
            sp.wait_ge(job_done, J_ROW)
            for u in range(3):
                load_x(0, u)
                if u < 2:
                    load_toep(0, u)

            def channel(k, u, loads=True):
                if loads or u < 1:
                    load_x(k + (u + 3) // 4, (u + 3) % 4)
                if loads or u < 2:
                    load_toep(k + (u + 2) // 4, (u + 2) % 4)
                store_x1(k, u)

            for u in range(4):
                channel(0, u)
            with sp.Fori(1, GROUPS - 1) as k:
                for u in range(4):
                    channel(k, u)
            for u in range(4):
                channel(GROUPS - 1, u, loads=False)
            for u in range(4):
                sp.wait_ge(x1_stored[u], 16 * GROUPS)
            sp.wait_ge(b2_stored, 16 * (AR // P))
            sp.wait_ge(c_stored, 16 * (AR // P + 1))

        @block.gpsimd
        def _(pool):
            made = [0]

            def const(ins):
                made[0] += 1
                ins.then_inc(consts, 1)
                pool.wait_ge(consts, made[0])

            const(nc.gpsimd.memset(ident[:], 0.0))
            const(nc.gpsimd.affine_select(ident[:], ident[:], pattern=[[-1, P]], base=0, channel_multiplier=1,
                                          compare_op=ALU.not_equal, fill=1.0))
            const(nc.gpsimd.iota(grid[:, 0, :], pattern=[[-G, G]], base=G * (G - 1), channel_multiplier=0,
                                 allow_small_or_imprecise_dtypes=True))
            const(nc.gpsimd.iota(grid[:, 1, :], pattern=[[-1, G]], base=G - 1, channel_multiplier=0,
                                 allow_small_or_imprecise_dtypes=True))
            const(nc.gpsimd.memset(last[:], 0.0))
            const(nc.gpsimd.affine_select(last[:], last[:], pattern=[[0, 1]], base=1 - G, channel_multiplier=1,
                                          compare_op=ALU.not_equal, fill=1.0))
            const(nc.gpsimd.memset(zero[:], 0.0))
            for half, turns3 in enumerate(((0.25, 0.5, 0.25), (0.5, 0.75, 0.0))):
                for j, turn in enumerate(turns3):
                    const(nc.gpsimd.memset(phase[64 * half:64 * half + 64, j:j + 1], turn))
                    const(nc.gpsimd.memset(phase[64 * half:64 * half + 64, 3 + j:4 + j], turn * TWO_PI))
            const(nc.gpsimd.iota(ramp[:], pattern=[[1, T]], base=0, channel_multiplier=0,
                                 allow_small_or_imprecise_dtypes=True))
            assert made[0] == CONSTS

            steps_done = [0]

            def link(ins):
                steps_done[0] += 1
                ins.then_inc(pchain, 1)
                pool.wait_ge(pchain, steps_done[0])

            pool.wait_ge(in_w3, 16)
            for c in range(K8):
                block_of = w3_raw[:, c, c * P:(c + 1) * P]
                ins = nc.gpsimd.tensor_tensor(block_of, block_of, ident[:], ALU.add)
            ins.then_inc(w3_ready, 1)

            def across(j):
                return part[:, j, :].unsqueeze(2).to_broadcast([P, C, G])

            def steps_of(j):
                return grid[:, j, :].unsqueeze(1).to_broadcast([P, C, G])

            tt = nc.gpsimd.tensor_tensor
            pool.wait_ge(part_ready, 1)
            tt(fac_v[:], across(1), steps_of(0), ALU.mult).then_inc(fac_turns, 1)
            tt(fac_t[:], across(0), steps_of(0), ALU.mult).then_inc(fac_decay, 1)
            pool.wait_ge(in_w2, 16)
            for c in range(K8):
                block_of = p2[:, c, c * P:(c + 1) * P]
                ins = tt(block_of, block_of, ident[:], ALU.add)
            ins.then_inc(p2_ready, 1)

            def stage_low(n):
                pool.wait_ge(staged_hi, n + 1)
                tt(staged[n % 2][:, 1], STAGES[n], f(staged[n % 2][:, 0]), ALU.subtract).then_inc(staged_lo, 1)

            stage_low(0)
            stage_low(1)
            pool.wait_ge(fac_exp, 1)
            pool.wait_ge(fac_sin, 1)
            link(tt(fac_u[:], fac_u[:], fac_t[:], ALU.mult))
            link(tt(fac_u[:], fac_u[:], across(2), ALU.mult))
            pool.wait_ge(fac_sin, 2)
            link(tt(fac_w[:], fac_w[:], fac_t[:], ALU.mult))
            stage_low(2)
            link(tt(fac_w[:], fac_w[:], across(3), ALU.mult))
            link(tt(fac_u[:], fac_u[:], fac_w[:], ALU.add))
            link(tt(fac_v[:], across(1), steps_of(1), ALU.mult))
            tt(fac_t[:], across(0), steps_of(1), ALU.mult).then_inc(fac_turns, 1)
            stage_low(3)
            pool.wait_ge(fac_exp, 2)
            pool.wait_ge(fac_sin, 3)
            tt(fac_v[:], fac_w[:], fac_t[:], ALU.mult).then_inc(factors, 1)

            pool.wait_ge(in_mix, 32)
            pool.wait_ge(factors, 1)
            for half in range(2):
                rows = slice(C * half, C * half + C)
                link(tt(mix[rows], mix[rows], ident[rows, C * half:C * half + C].unsqueeze(1).to_broadcast([C, S1, C]), ALU.add))
            for n in range(4, len(STAGES)):
                if n == K8:
                    pool.wait_ge(in_b2, 16 * K8)
                stage_low(n)

            def toep_low(k, u):
                h = 4 * k + u
                pool.wait_ge(toep_hi, h + 1)
                nc.gpsimd.tensor_tensor(toep[u % 2][:, 1], toep_raw[u % 2][:, ::-1], f(toep[u % 2][:, 0]),
                                        ALU.subtract).then_inc(toep_lo, 1)

            over_channels(pool, toep_low)

        @block.scalar
        def _(act):
            def trig(to, scale, bias):
                nc.scalar.activation(to, to, ACT.Sin, scale=scale, bias=bias).then_inc(fac_sin, 1)

            act.wait_ge(trig_in, 1)
            nc.scalar.activation(sin1[:], frac[:], ACT.Sin, scale=TWO_PI).then_inc(trig_out, 1)
            nc.scalar.activation(sinh[:], frac[:], ACT.Sin, scale=TWO_PI / 2).then_inc(trig_out, 1)

            def high(j, to, of):
                act.wait_ge(job_done, j + 1)
                nc.scalar.activation(to, of, ACT.Copy).then_inc(job_hi, 1)

            def stage_high(n):
                if n >= 2:
                    act.wait_ge(job_done, STAGE_JOBS[n - 2] + 1)
                nc.scalar.activation(staged[n % 2][:, 0], STAGES[n], ACT.Copy).then_inc(staged_hi, 1)

            for i in range(K8):
                high(J_W3 + i, p3[:, 0, i, :], ps[(J_W3 + i) % 4][:])
            act.wait_ge(p2_ready, 1)
            act.wait_ge(job_done, J_W3)
            act.wait_ge(part_ready, 1)
            act.wait_ge(kern_stored, 16)
            stage_high(0)
            stage_high(1)
            act.wait_ge(fac_decay, 1)
            nc.scalar.activation(fac_t[:], fac_t[:], ACT.Exp).then_inc(fac_exp, 1)
            act.wait_ge(fac_arg, 1)
            trig(fac_u[:], -TWO_PI, phase[:, 3:4])
            act.wait_ge(fac_arg, 2)
            trig(fac_w[:], -TWO_PI, phase[:, 4:5])
            act.wait_ge(bias_ready, 1)
            for i in range(half_t):
                high(J_D0 + i, dense0[:, 0, i, :], ps[(J_D0 + i) % 4][:])
                stage_high(i + 2)
                if i == 1:
                    act.wait_ge(fac_arg, 3)
                    trig(fac_w[:], -TWO_PI, phase[:, 5:6])
                    nc.scalar.activation(fac_t[:], fac_t[:], ACT.Exp).then_inc(fac_exp, 1)
            act.wait_ge(kern_stored, 32)
            for i in range(half_t):
                high(J_D1 + i, dense1[:, 0, i, :], ps[(J_D1 + i) % 4][:])
                if half_t + i + 2 == K8:
                    act.wait_ge(in_b2, 16 * K8)
                stage_high(half_t + i + 2)
            for m in range(AR // P):
                act.wait_ge(job_done, J_B2 + m + 1)
                if m >= 1:
                    act.wait_ge(b2_stored, 16 * m)
                else:
                    act.wait_ge(job_done, J_A3 + K8)
                nc.scalar.activation(b2_out[:, 0], ps[(J_B2 + m) % 4][:], ACT.Copy).then_inc(b2_hi, 1)
                if m + K8 + 2 < len(STAGES):
                    stage_high(m + K8 + 2)

            def split_high(k, u):
                h = 4 * k + u
                act.wait_ge(toep_in[u % 2], 32 * k + 16 * (u // 2) + 16)
                ready(act, conv_done, h - 1)
                nc.scalar.activation(toep[u % 2][:, 0], toep_raw[u % 2][:, ::-1], ACT.Copy).then_inc(toep_hi, 1)
                act.wait_ge(ut_ps, h + 1)
                nc.scalar.activation(ut[u % 2][:, 0], ps[u % 2][:].rearrange("p (i b) -> p i b", i=K8),
                                     ACT.Copy).then_inc(ut_hi, 1)

            over_channels(act, split_high)

        @block.vector
        def _(dve):
            count = [0]

            def link(ins):
                count[0] += 1
                ins.then_inc(chain, 1)
                dve.wait_ge(chain, count[0])

            tt, ts, stt = nc.vector.tensor_tensor, nc.vector.tensor_scalar, nc.vector.scalar_tensor_tensor

            def exp_parts(z, k, r, q, two_k, ki):
                link(ts(k, z, LOG2E, ROUND, ALU.mult, ALU.add))
                link(ts(k, k, ROUND, -126.0, ALU.subtract, ALU.max))
                link(ts(k, k, 127.0, None, ALU.min))
                link(stt(r, k, -LN2_HI, z, ALU.mult, ALU.add))
                link(stt(r, k, -LN2_LO, r, ALU.mult, ALU.add))
                link(ts(q, r, 1.0 / 40320, None, ALU.mult))
                for n in (5040, 720, 120, 24, 6, 2, 1):
                    link(stt(q, q, 1.0 / n, r, ALU.add, ALU.mult))
                link(ts(ki, k, 127.0, None, ALU.add))
                link(ts(two_k.bitcast(I32), ki, 23, None, ALU.logical_shift_left))

            dve.wait_ge(in_small, 16 * SMALL)
            exp_parts(logs[:], e_k[:], e_f[:], e_q[:], e_2k[:], e_i[:])
            link(tt(e_q[:], e_q[:], e_2k[:], ALU.mult))
            link(tt(exps[:], e_q[:], e_2k[:], ALU.add))
            ar, dt = exps[:, 0:N], exps[:, N:N + 1]
            link(ts(decay[:], ar, dt, -1.0, ALU.mult, ALU.mult))
            link(ts(angle[:], aim[:], dt, None, ALU.mult))
            link(ts(turns[:], angle[:], 1.0 / (2 * math.pi), None, ALU.mult))
            link(ts(tmp[:], turns[:], ROUND, ROUND, ALU.add, ALU.subtract))
            dve.wait_ge(chain, count[0])
            tt(frac[:], turns[:], tmp[:], ALU.subtract).then_inc(trig_in, 1)
            exp_parts(decay[:], e_k[:, 0:N], e_f[:, 0:N], e_q[:, 0:N], e_2k[:, 0:N], e_i[:, 0:N])
            link(tt(e_q[:, 0:N], e_q[:, 0:N], e_2k[:, 0:N], ALU.mult))
            link(ts(e_f[:, 0:N], e_2k[:, 0:N], 1.0, None, ALU.subtract))
            link(tt(em1[:], e_q[:, 0:N], e_f[:, 0:N], ALU.add))
            dve.wait_ge(trig_out, 2)
            link(tt(tmp[:], sinh[:], sinh[:], ALU.mult))
            link(ts(cosm1[:], tmp[:], -2.0, None, ALU.mult))
            link(stt(zr[:], cosm1[:], 1.0, em1[:], ALU.add, ALU.mult))
            link(tt(zr[:], zr[:], cosm1[:], ALU.add))
            link(stt(zi[:], em1[:], 1.0, sin1[:], ALU.add, ALU.mult))
            link(tt(tmp[:], ar, ar, ALU.mult))
            link(tt(den[:], aim[:], aim[:], ALU.mult))
            link(tt(den[:], den[:], tmp[:], ALU.add))
            link(nc.vector.reciprocal(den[:], den[:]))
            link(tt(nr[:], zi[:], aim[:], ALU.mult))
            link(tt(tmp[:], zr[:], ar, ALU.mult))
            link(tt(nr[:], nr[:], tmp[:], ALU.subtract))
            link(stt(nr[:], nr[:], 2.0, den[:], ALU.mult, ALU.mult))
            link(tt(ni[:], zr[:], aim[:], ALU.mult))
            link(tt(tmp[:], zi[:], ar, ALU.mult))
            link(tt(ni[:], ni[:], tmp[:], ALU.add))
            link(stt(ni[:], ni[:], -2.0, den[:], ALU.mult, ALU.mult))
            c3 = cri[:].rearrange("h (n c) -> h n c", c=2)
            p4 = par[:].rearrange("h (j d n) -> h j d n", j=4, d=2)
            def both(j):
                return p4[:, j, :, :]
            def twice(t):
                return t[:].unsqueeze(1).to_broadcast([C, 2, N])
            link(nc.vector.tensor_copy(both(0), twice(decay)))
            link(nc.vector.tensor_copy(both(1), twice(turns)))
            link(tt(tmp[:], nr[:], c3[:, :, 0], ALU.mult))
            link(tt(tmp2[:], ni[:], c3[:, :, 1], ALU.mult))
            link(tt(both(2), twice(tmp), twice(tmp2), ALU.subtract))
            link(tt(tmp[:], nr[:], c3[:, :, 1], ALU.mult))
            link(tt(tmp2[:], ni[:], c3[:, :, 0], ALU.mult))
            link(tt(both(3), twice(tmp), twice(tmp2), ALU.add))
            nc.vector.tensor_copy(lens[:], lens_i[:]).then_inc(base_ready, 1)
            dve.wait_ge(base_ready, 1)
            dve.wait_ge(consts, CONSTS)
            link(ts(mask[:], ramp[:], lens[:], None, ALU.is_lt))
            mask_made = count[0]
            dve.wait_ge(job_done, J_PAR + 1)
            link(nc.vector.tensor_copy(part[:], ps[0][:, 0:4 * C].rearrange("p (j h) -> p j h", j=4)))
            nc.vector.tensor_copy(bias_col[:], ps[0][:, 4 * C:4 * C + K8]).then_inc(part_ready, 1)
            dve.wait_ge(part_ready, 1)

            highs = [0]

            def low(j, to, of, high):
                highs[0] += 1
                dve.wait_ge(job_hi, highs[0])
                tt(to, of, f(high), ALU.subtract).then_inc(job_free, 1)

            def reduced(to, of, j):
                link(ts(to, of, phase[:, j:j + 1], ROUND, ALU.add, ALU.add))
                stt(to, to, ROUND, of, ALU.subtract, ALU.subtract).then_inc(fac_arg, 1)

            low(J_W3, p3[:, 1, 0, :], ps[J_W3 % 4][:], p3[:, 0, 0, :])
            low(J_W3 + 1, p3[:, 1, 1, :], ps[(J_W3 + 1) % 4][:], p3[:, 0, 1, :])
            dve.wait_ge(fac_turns, 1)
            reduced(fac_u[:], fac_v[:], 0)
            for i in range(2, 5):
                low(J_W3 + i, p3[:, 1, i, :], ps[(J_W3 + i) % 4][:], p3[:, 0, i, :])
            reduced(fac_w[:], fac_v[:], 1)
            for i in range(5, K8):
                low(J_W3 + i, p3[:, 1, i, :], ps[(J_W3 + i) % 4][:], p3[:, 0, i, :])
            dve.wait_ge(in_bias, 16)
            dve.wait_ge(w3_ready, 1)
            for c in range(K8):
                link(nc.vector.tensor_tensor_reduce(out=waste[:], in0=w3_raw[:, c, :], in1=b3t[:], scale=1.0, scalar=0.0,
                                                    op0=ALU.mult, op1=ALU.add, accum_out=bias_p3[:, c:c + 1]))
            nc.vector.memset(waste[:, 0:1], 0.0).then_inc(bias_ready, 1)
            for i in range(half_t):
                low(J_D0 + i, dense0[:, 1, i, :], ps[(J_D0 + i) % 4][:], dense0[:, 0, i, :])
                if i == 0:
                    dve.wait_ge(fac_turns, 2)
                    reduced(fac_w[:], fac_v[:], 2)
            for i in range(2):
                j = J_K + i
                dve.wait_ge(job_done, j + 1)
                nc.vector.tensor_copy(kern[:, i * C // 2:(i + 1) * C // 2, :],
                                      ps[j % 4][0:G, :].rearrange("q (h r) -> q h r", r=G)).then_inc(job_free, 1)
            dve.wait_ge(job_free, J_K + 1)
            link(ts(dcol[:], dcol[:], 1.0, last[:], ALU.add, ALU.mult))
            tt(kern[:, :, G - 1], kern[:, :, G - 1], dcol[:], ALU.add).then_inc(kern_ready, 1)
            for i in range(half_t):
                low(J_D1 + i, dense1[:, 1, i, :], ps[(J_D1 + i) % 4][:], dense1[:, 0, i, :])

            def copied(j, to, of, scale=None):
                dve.wait_ge(job_done, j + 1)
                if scale is None:
                    return nc.vector.tensor_copy(to, of)
                return ts(to, of, scale, None, ALU.mult)

            for i in range(K8):
                copied(J_A3 + i, lora3_in[:, i, :], ps[(J_A3 + i) % 4][:, 0:LR]).then_inc(job_free, 1)
            for m in range(AR // P + 1):
                rows = P if m < AR // P else 1
                copied(J_C + m, c_out[m][0:rows], ps[(J_C + m) % 4][0:rows, 0:LR]).then_inc(job_free, 1)
            for m in range(AR // P):
                dve.wait_ge(b2_hi, m + 1)
                tt(b2_out[:, 1], ps[(J_B2 + m) % 4][:], f(b2_out[:, 0]), ALU.subtract).then_inc(job_free, 1)
            copied(J_ROW, bias_row[:], ps[J_ROW % 4][0:1, :]).then_inc(job_free, 1)
            copied(J_ROW + 1, b3t[:], ps[(J_ROW + 1) % 4][:], 0.5).then_inc(job_free, 1)
            for i in range(K8):
                copied(J_LA + i, lora2_in[:, i, :], ps[(J_LA + i) % 4][:, 0:AR]).then_inc(job_free, 1)

            def transposed_low(k, u):
                dve.wait_ge(ut_hi, 4 * k + u + 1)
                tt(ut[u % 2][:, 1], ps[u % 2][:].rearrange("p (i b) -> p i b", i=K8), f(ut[u % 2][:, 0]),
                   ALU.subtract).then_inc(ut_lo, 1)

            def masked(k, u):
                dve.wait_ge(conv_done, 4 * k + u + 1)
                dve.sem_inc(mask_begun, 1)
                dve.wait_ge(chain, mask_made)
                nc.vector.copy_predicated(xt[u][:], mask[:], ps[2 + u % 2][:]).then_inc(x1_ready, 1)

            def channel(k, u, ahead=True):
                if ahead:
                    transposed_low(k + (u + 1) // 4, (u + 1) % 4)
                masked(k, u)

            transposed_low(0, 0)
            with dve.Fori(0, GROUPS - 1) as k:
                for u in range(4):
                    channel(k, u)
            for u in range(4):
                channel(GROUPS - 1, u, ahead=u < 3)

        @block.tensor
        def _(pe):
            mm = nc.tensor.matmul

            def job(j):
                if j > 4:
                    pe.wait_ge(job_free, j - 4)
                return ps[j % 4]

            def over_chunks(out_ap, lhs, rhs):
                for i in range(K8):
                    ins = mm(out_ap, lhs(i), rhs(i), start=i == 0, stop=i == K8 - 1)
                return ins

            pe.wait_ge(base_ready, 1)
            pe.wait_ge(consts, 2)
            pe.wait_ge(in_small, 16 * SMALL)
            t = job(J_PAR)
            for q in range(4):
                nc.tensor.transpose(t[:, q * C:(q + 1) * C], par[:, q * 2 * N:(q + 1) * 2 * N], ident[0:C, 0:C])
            nc.tensor.transpose(t[:, 4 * C:4 * C + K8], bias8[:], ident[0:K8, 0:K8]).then_inc(job_done, 1)
            pe.wait_ge(part_ready, 1)

            pe.wait_ge(w3_ready, 1)
            for i in range(K8):
                t = job(J_W3 + i)
                for c in range(K8):
                    ins = nc.tensor.transpose(t[:, c * P:(c + 1) * P], w3_raw[:, c, i * P:(i + 1) * P], ident[:])
                ins.then_inc(job_done, 1)

            stages = [0]

            def split_job(j):
                n = stages[0]
                stages[0] += 1
                t = job(j)
                pe.wait_ge(staged_lo, n + 1)
                for half in range(2):
                    cols = slice(half * HB, (half + 1) * HB)
                    for c in range(K8):
                        for a, b in ((0, 0), (0, 1), (1, 0)):
                            ins = mm(t[:, cols], staged[n % 2][:, a, c, :], p3[:, b, c, cols],
                                     start=c == a == b == 0, stop=c == K8 - 1 and a == 1)
                ins.then_inc(job_done, 1)

            pe.wait_ge(job_free, J_W3 + K8 - 1)
            for i in range(half_t):
                split_job(J_D0 + i)
            pe.wait_ge(factors, 1)
            for q in range(2):
                t = job(J_K + q)
                for h in range(C // 2):
                    c = q * C // 2 + h
                    ins = mm(t[0:G, h * G:(h + 1) * G], fac_u[:, c, :], fac_v[:, c, :], start=True, stop=True)
                ins.then_inc(job_done, 1)
            for i in range(half_t):
                split_job(J_D1 + i)
            pe.wait_ge(in_a3, 16 * K8)
            for i in range(K8):
                t = job(J_A3 + i)
                over_chunks(t[:, 0:LR], lambda c: p2[:, c, i * P:(i + 1) * P], lambda c: a3raw[:, c, :]).then_inc(job_done, 1)
            pe.wait_ge(in_b2, 16 * K8)
            for m in range(AR // P):
                t = job(J_C + m)
                over_chunks(t[:, 0:LR], lambda c: b2raw[:, c, m * P:(m + 1) * P], lambda c: a3raw[:, c, :]).then_inc(job_done, 1)
            t = job(J_C + AR // P)
            over_chunks(t[0:1, 0:LR], lambda c: bias_col[:, c:c + 1], lambda c: a3raw[:, c, :]).then_inc(job_done, 1)
            for m in range(AR // P):
                split_job(J_B2 + m)
            t = job(J_ROW)
            pe.wait_ge(bias_ready, 1)
            for c in range(K8):
                ins = mm(t[0:1, c * P:(c + 1) * P], bias_p3[:, c:c + 1], ident[:], start=True, stop=True)
            ins.then_inc(job_done, 1)
            t = job(J_ROW + 1)
            pe.wait_ge(in_b3, 16 * 4)
            for c in range(K8):
                ins = nc.tensor.transpose(t[:, c * P:(c + 1) * P], b3rep[:, c, :, :].rearrange("p a r -> p (a r)"), ident[:])
            ins.then_inc(job_done, 1)
            pe.wait_ge(in_la, 16)
            for i in range(K8):
                t = job(J_LA + i)
                for c in range(AR // P):
                    ins = nc.tensor.transpose(t[:, c * P:(c + 1) * P], lora_a_raw[:, c, i * P:(i + 1) * P], ident[:])
                ins.then_inc(job_done, 1)

            def transpose_x(k, u):
                h = 4 * k + u
                pe.wait_ge(x_in[u], 16 * k + 16)
                ready(pe, ut_lo, h - 1)
                for i in range(K8):
                    ins = nc.tensor.transpose(ps[u % 2][:, i * P:(i + 1) * P], xt[u][:, i * P:(i + 1) * P], ident[:])
                ins.then_inc(ut_ps, 1)

            def convolve(k, u):
                h = 4 * k + u
                pe.wait_ge(toep_lo, h + 1)
                pe.wait_ge(ut_lo, h + 1)
                ready(pe, x1_ready, h - 1)
                y, xs, tp = ps[2 + u % 2], ut[u % 2], toep[u % 2]
                for i in range(K8):
                    for a in range(2):
                        for b in range(2 - a):
                            for bank in range(2):
                                lo, hi = max(i * P, bank * HB), (bank + 1) * HB
                                if lo < hi:
                                    ins = mm(y[:, lo:hi], xs[:, a, i, :], tp[:, b, lo - i * P:hi - i * P],
                                             start=i == 0 and a == 0 and b == 0,
                                             stop=a == 1 and i == (bank + 1) * half_t - 1)
                ins.then_inc(conv_done, 1)

            pe.wait_ge(job_free, JOBS - 1)
            transpose_x(0, 0)

            def channel(k, u, ahead=True):
                if ahead:
                    transpose_x(k + (u + 1) // 4, (u + 1) % 4)
                convolve(k, u)

            for u in range(4):
                channel(0, u)
            with pe.Fori(1, GROUPS - 1) as k:
                for u in range(4):
                    channel(k, u)
            for u in range(4):
                channel(GROUPS - 1, u, ahead=u < 3)


    x1_landed = [sem(f"x1_landed{i}") for i in range(2)]
    stack_landed = [sem(f"stack_landed{i}") for i in range(2)]
    y_stored = [sem(f"y_stored{i}") for i in range(2)]
    gathered_m, gathered_a = sem("gathered_m"), sem("gathered_a")
    x2_ps, x2_copied, x2_hi, x2_lo = (sem(f"x2_{n}") for n in ("ps", "copied", "hi", "lo"))
    h2_ps, h2_ready = sem("h2_ps"), sem("h2_ready")
    h_ps, h_sum, h_hi, h_lo = sem("h_ps"), sem("h_sum"), sem("h_hi"), sem("h_lo")
    c_landed = [sem(f"c_landed{i}") for i in range(2)]
    c_zeroed = sem("c_zeroed")
    y_ps, y_left, y_right = sem("y_ps"), sem("y_left"), sem("y_right")
    fixed, gfixed = sem("fixed"), sem("gfixed")
    PAIRS = TILES // 2
    c_adapters = c_d[0:AR].rearrange("(a r) c -> a r c", r=R2)
    x1_rows = x1_d.rearrange("(n b) c t -> n (b c) t", b=2)
    out_rows = out.rearrange("(n b) c t -> n (b c) t", b=2)

    def over_tiles(eng, body):
        for v in range(2):
            body(0, v)
        with eng.Fori(1, PAIRS - 1) as k:
            for v in range(2):
                body(k, v)
        for v in range(2):
            body(PAIRS - 1, v)

    def exists(k, v):
        return not isinstance(k, int) or 2 * k + v < TILES

    with nc.Block() as block:
        @block.sync
        def _(sp):
            def load_x1(k, v):
                k, v = k + v // 2, v % 2
                n = 2 * k + v
                ready(sp, x2_ps, n - 1)
                sp.dma_start(x1_in[v][:], x1_rows[bass.ds(n, 1)].squeeze(0)).then_inc(x1_landed[v], 16)

            def load_stack(k, v):
                k, v = k + v // 2, v % 2
                n = 2 * k + v
                ready(sp, y_ps, n - 1)
                for b in range(2):
                    a = sp.value_load(index[0:1, bass.ds(2 * n + b + B, 1)], min_val=0, max_val=A2N - 1)
                    l = sp.value_load(index[0:1, bass.ds(2 * n + b + 2 * B, 1)], min_val=0, max_val=L3N - 1)
                    rows = slice(b * R2, (b + 1) * R2)
                    cols = slice(2 * R2 + b * R3, 2 * R2 + (b + 1) * R3)
                    sp.dma_start(f(stack[v][rows]), b2_d[bass.ds(a, 1)].squeeze(0)).then_inc(stack_landed[v], 16)
                    sp.dma_start(c_gath[v][rows, cols], c_adapters[bass.ds(a, 1), :, bass.ds(l * R3, R3)].squeeze(0)).then_inc(c_landed[v], 16)
                    sp.dma_start(c_gath[v][2 * R2 + b:2 * R2 + b + 1, cols], c_d[AR:AR + 1, bass.ds(l * R3, R3)]).then_inc(c_landed[v], 16)

            def tile(k, v):
                if exists(k, v + 2):
                    load_x1(k, v + 2)
                n = 2 * k + v
                sp.wait_ge(y_left, n + 1)
                sp.wait_ge(y_right, n + 1)
                sp.dma_start(out_rows[bass.ds(n, 1)].squeeze(0), y_out[v][:]).then_inc(y_stored[v], 16)
                if exists(k, v + 2):
                    load_stack(k, v + 2)

            for v in range(2):
                load_x1(0, v)
            sp.wait_ge(c_zeroed, 2)
            for v in range(2):
                load_stack(0, v)
            over_tiles(sp, tile)
            for v in range(2):
                sp.wait_ge(y_stored[v], 16 * PAIRS)

        @block.gpsimd
        def _(pool):
            for v in range(2):
                nc.gpsimd.memset(m_gath[v][:], 0.0).then_inc(gfixed, 1)
            for v in range(2):
                nc.gpsimd.memset(c_gath[v][:], 0.0).then_inc(c_zeroed, 1)
            pool.wait_ge(gfixed, 2)
            pool.wait_ge(c_zeroed, 2)

            def gather(k, v):
                k, v = k + v // 2, v % 2
                n = 2 * k + v
                ready(pool, x2_ps, n - 1)
                for b in range(2):
                    s = pool.value_load(index[0:1, bass.ds(2 * n + b, 1)], min_val=0, max_val=S1 - 1)
                    rows = slice(b * C, (b + 1) * C)
                    ins = nc.gpsimd.tensor_copy(m_gath[v][rows, b * C:(b + 1) * C], mix[rows, bass.ds(s, 1), :].squeeze(1))
                ins.then_inc(gathered_m, 1)
                pool.wait_ge(gathered_m, n + 1)
                ready(pool, h2_ps, n - 1)
                for b in range(2):
                    a = pool.value_load(index[0:1, bass.ds(2 * n + b + B, 1)], min_val=0, max_val=A2N - 1)
                    l = pool.value_load(index[0:1, bass.ds(2 * n + b + 2 * B, 1)], min_val=0, max_val=L3N - 1)
                    nc.gpsimd.tensor_copy(a_gath[v][:, :, b * R2:(b + 1) * R2], lora2_in[:, :, bass.ds(a * R2, R2)])
                    c = 2 * R2 + b * R3
                    ins = nc.gpsimd.tensor_copy(a_gath[v][:, :, c:c + R3], lora3_in[:, :, bass.ds(l * R3, R3)])
                ins.then_inc(gathered_a, 1)
                pool.wait_ge(gathered_a, n + 1)

            for v in range(2):
                gather(0, v)

            def tile(k, v):
                if exists(k, v + 2):
                    gather(k, v + 2)

            over_tiles(pool, tile)

        @block.scalar
        def _(act):
            def x2_high(k, v):
                k, v = k + v // 2, v % 2
                n = 2 * k + v
                act.wait_ge(x2_copied, n + 1)
                ready(act, y_ps, n - 1)
                nc.scalar.activation(x2t[v][:, 0], x2f[v][:], ACT.Copy).then_inc(x2_hi, 1)

            def tile(k, v):
                if exists(k, v + 1):
                    x2_high(k, v + 1)
                n = 2 * k + v
                act.wait_ge(y_ps, n + 1)
                if not isinstance(k, int) or k > 0:
                    act.wait_ge(y_stored[v], 16 * k)
                nc.scalar.activation(y_out[v][:, 0:HB], ps[2 + v][:, 0:HB], ACT.Copy).then_inc(y_left, 1)

            x2_high(0, 0)
            over_tiles(act, tile)

        @block.vector
        def _(dve):
            tt = nc.vector.tensor_tensor
            made = [0]

            def fix(ins):
                made[0] += 1
                ins.then_inc(fixed, 1)
                dve.wait_ge(fixed, made[0])

            fix(nc.vector.memset(hmask[:], 0.0))
            fix(nc.vector.memset(hmask[0:R2, 0:C], 1.0))
            fix(nc.vector.memset(hmask[2 * R2:2 * R2 + R3, 0:C], 1.0))
            fix(nc.vector.memset(hmask[2 * R2 + R3:KR, C:P], 1.0))
            fix(nc.vector.tensor_reduce(hm[0][0:2 * R2, 0:1], ident[0:2 * R2, R2:2 * R2], mybir.AxisListType.X, ALU.add))
            fix(nc.vector.tensor_copy(hmask[0:2 * R2, C:P], hm[0][0:2 * R2, 0:1].to_broadcast([2 * R2, C])))
            for v in range(2):
                for b in range(2):
                    fix(nc.vector.tensor_copy(hc[v][2 * R2:KC, b * C:(b + 1) * C],
                                              ident[2 * R2:KC, 2 * R2 + b:2 * R2 + b + 1].to_broadcast([2, C])))
                fix(nc.vector.memset(f(hs[v][KR:KR + 1, 0]), 1.0))
                fix(nc.vector.memset(f(hs[v][KR:KR + 1, 1]), 0.0))
                for rows, of in ((slice(2 * R2, 2 * R2 + R3), b3t[2 * R2:2 * R2 + R3]),
                                 (slice(2 * R2 + R3, KR), b3t[2 * R2 + R3:KR]), (slice(KR, KR + 1), bias_row[:])):
                    fix(nc.vector.tensor_copy(stack[v][rows, 0], of))
                    fix(tt(stack[v][rows, 1], of, f(stack[v][rows, 0]), ALU.subtract))

            def x2_copy(k, v):
                k, v = k + v // 2, v % 2
                n = 2 * k + v
                dve.wait_ge(x2_ps, n + 1)
                ready(dve, h2_ps, n - 1)
                nc.vector.tensor_copy(x2f[v][:], ps[0][:].rearrange("p (i m) -> p i m", i=K8)).then_inc(x2_copied, 1)
                dve.wait_ge(x2_hi, n + 1)
                tt(x2t[v][:, 1], x2f[v][:], f(x2t[v][:, 0]), ALU.subtract).then_inc(x2_lo, 1)

            def adapter_inputs(k, v):
                n = 2 * k + v
                dve.wait_ge(h2_ps, n + 1)
                ready(dve, h_ps, n - 1)
                low = ps[1][0:KR, v * HB:v * HB + P]
                tt(hm[v][:], low, hmask[:], ALU.mult).then_inc(h_sum, 1)
                tt(hc[v][0:2 * R2], low[0:2 * R2], hmask[0:2 * R2], ALU.mult).then_inc(h2_ready, 1)

            def low_rank(k, v):
                n = 2 * k + v
                dve.wait_ge(h_ps, n + 1)
                ready(dve, y_ps, n - 1)
                dve.wait_ge(h_sum, 2 * n + 1)
                tt(hm[v][:], hm[v][:], ps[1][0:KR, v * HB + P:v * HB + 2 * P], ALU.add).then_inc(h_sum, 1)
                dve.wait_ge(h_sum, 2 * n + 2)
                nc.vector.tensor_copy(hs[v][0:KR, 0], hm[v][:]).then_inc(h_hi, 1)
                dve.wait_ge(h_hi, n + 1)
                tt(hs[v][0:KR, 1], hm[v][:], f(hs[v][0:KR, 0]), ALU.subtract).then_inc(h_lo, 1)

            def tile(k, v):
                if exists(k, v + 1):
                    x2_copy(k, v + 1)
                adapter_inputs(k, v)
                low_rank(k, v)
                n = 2 * k + v
                dve.wait_ge(y_ps, n + 1)
                if not isinstance(k, int) or k > 0:
                    dve.wait_ge(y_stored[v], 16 * k)
                nc.vector.tensor_copy(y_out[v][:, HB:T], ps[2 + v][:, HB:T]).then_inc(y_right, 1)

            x2_copy(0, 0)
            over_tiles(dve, tile)

        @block.tensor
        def _(pe):
            mm = nc.tensor.matmul
            PASSES = ((0, 0), (0, 1), (1, 0))

            def mixing(k, v):
                k, v = k + v // 2, v % 2
                n = 2 * k + v
                pe.wait_ge(x1_landed[v], 16 * k + 16)
                pe.wait_ge(gathered_m, n + 1)
                ready(pe, x2_copied, n)
                for i in range(K8):
                    ins = mm(ps[0][:, i * P:(i + 1) * P], x1_in[v][:, i * P:(i + 1) * P], m_gath[v][:], start=True, stop=True)
                ins.then_inc(x2_ps, 1)

            def low_rank(k, v):
                n = 2 * k + v
                pe.wait_ge(x2_copied, n + 1)
                pe.wait_ge(gathered_a, n + 1)
                ready(pe, h_sum, 2 * n - 2)
                for i in range(K8):
                    ins = mm(ps[1][0:KR, v * HB:v * HB + P], a_gath[v][:, i, :], x2f[v][:, i, :],
                             start=i == 0, stop=i == K8 - 1)
                ins.then_inc(h2_ps, 1)

            def adapters(k, v):
                pe.wait_ge(c_landed[v], 64 * k + 64)
                pe.wait_ge(h2_ready, 2 * k + v + 1)
                if isinstance(k, int) and k == 0:
                    pe.wait_ge(fixed, FIXED)
                mm(ps[1][0:KR, v * HB + P:v * HB + 2 * P], c_gath[v][:], hc[v][:], start=True, stop=True).then_inc(h_ps, 1)

            def dense(k, v):
                n = 2 * k + v
                ready(pe, y_left, n - 1)
                ready(pe, y_right, n - 1)
                pe.wait_ge(x2_lo, n + 1)
                y = ps[2 + v]
                for i in range(K8):
                    w = (dense0, dense1)[i // half_t]
                    for a in range(2):
                        for b in range(2 - a):
                            for half in range(2):
                                cols = slice(half * HB, (half + 1) * HB)
                                mm(y[:, cols], x2t[v][:, a, i, :], w[:, b, i % half_t, cols],
                                   start=i == 0 and a == b == 0, stop=False)
                    if i == 1:
                        adapters(k, v)
                pe.wait_ge(h_lo, n + 1)
                pe.wait_ge(stack_landed[v], 32 * k + 32)
                for a in range(2):
                    for b in range(2 - a):
                        for half in range(2):
                            cols = slice(half * HB, (half + 1) * HB)
                            ins = mm(y[:, cols], hs[v][:, a, :], stack[v][:, b, cols], start=False, stop=a == 1)
                ins.then_inc(y_ps, 1)

            def tile(k, v):
                if exists(k, v + 1):
                    mixing(k, v + 1)
                low_rank(k, v)
                dense(k, v)

            mixing(0, 0)
            over_tiles(pe, tile)


_INS = ["x", "itok_B_8_3872", "itok_B_0_15", "itok_B_6_15", "itok_B_0_2", "L0_cond_log_dt", "L0_cond_C",
        "L0_cond_log_A_real", "L0_cond_A_imag", "L0_cond_D", "L1_cond_weights", "L2_cond_base_weight",
        "L2_cond_base_bias", "L2_cond_lora_A_w", "L2_cond_lora_B_w", "L3_cond_W", "L3_cond_lora_A", "L3_cond_lora_B_w"]


def kernel(**inputs):
    import numpy as np
    from concourse import bacc
    from concourse.bass_utils import run_bass_kernel_spmd

    nc = bacc.Bacc("TRN2", target_bir_lowering=False, num_devices=1, dynamic_dma_scratch_size=1024)
    arrays, args = {}, []
    for name in _INS:
        a = np.ascontiguousarray(inputs[name])
        arrays[f"in_{name}"] = a
        args.append(nc.dram_tensor(f"in_{name}", a.shape, mybir.dt.from_np(a.dtype), kind="ExternalInput").ap())
    args.append(nc.dram_tensor("out_0", (B, C, T), F32, kind="ExternalOutput").ap())
    program(nc, *args)
    r = run_bass_kernel_spmd(nc, [arrays], core_ids=[0])
    return r.results[0]["out_0"]
```

```python
import math

import concourse.bass as bass
from concourse import mybir

F32, F32R = mybir.dt.float32, mybir.dt.float32r
I32, U8 = mybir.dt.int32, mybir.dt.uint8
ALU = mybir.AluOpType
ACT = mybir.ActivationFunctionType

B, C, T = 128, 64, 1024
N = 64
P = 128
K8 = T // P
S1 = 16
A2N, R2 = 32, 16
L3N, R3 = 5, 32
AR, LR = A2N * R2, L3N * R3
G = 32
HB = T // 2
TILES = B // 2
KR = 2 * R2 + 2 * R3
KS = 2 * R2 + R3
KC = 2 * R2 + 2
ROUND = 1.5 * 2.0 ** 23
TWO_PI = 6.283184
LOG2E = 1.4426950408889634
LN2_HI, LN2_LO = 0.693145751953125, 1.4286068203094172e-06
WT = T + KR
GW = 3 * P
GROUPS_OF = ((0, GW), (GW, 2 * GW), (2 * GW, WT))
TAIL = T - 2 * GW
QT = T // 4
TOEP = 3 * QT
TFOLD = 3 * QT - P
RAW0 = TOEP + TFOLD - T
LAYOUT_END = 229368


def program(nc, x, steps, cond, adapter, labeler, log_dt, ssm_c, log_a_real, a_imag, ssm_d,
            mix_w, w2, bias2, lora2_a, lora2_b, w3, lora3_a, lora3_b, out):
    base = (nc.sbuf_base + 63) // 64 * 64

    def at(name, shape, dtype, offset):
        size = math.prod(shape[1:]) * mybir.dt.size(dtype)
        assert base + offset + size <= LAYOUT_END, (name, base + offset + size)
        return nc.alloc_sbuf_tensor_at(name, shape, dtype, offset=base + offset), (offset + size + 31) // 32 * 32

    half_t = K8 // 2
    dense0, o_dense1 = at("dense0", [P, 2, half_t, WT], F32R, 0)
    dense1, o_lora2 = at("dense1", [P, 2, half_t, WT], F32R, o_dense1)
    lora2_in, o = at("lora2_in", [P, K8, AR], F32, o_lora2)
    lora3_in, o = at("lora3_in", [P, K8, LR], F32, o)
    mix, o = at("mix", [P, S1, C], F32, o)
    b3t, o = at("b3t", [P, T], F32, o)
    B3_ROWS = slice(2 * R2, KS)
    ident, o = at("ident", [P, P], F32, o)
    index, o = at("index", [1, 3 * B], I32, o)
    mask, o_phase = at("mask", [P, T], U8, o)

    w3_raw, o = at("w3_raw", [P, K8, T], F32, 0)
    assert o <= o_dense1
    fac_u, o = at("fac_u", [P, C, G], F32, o_dense1)
    fac_v, o_fac_w = at("fac_v", [P, C, G], F32, o)
    fac_w, o_fac_t = at("fac_w", [P, C, G], F32, o_fac_w)
    fac_t, o = at("fac_t", [P, C, G], F32, o_fac_t)
    kern, _ = at("kern", [G, C, G], F32, o_fac_t)
    ramp, _ = at("ramp", [P, T], F32, o_fac_t)
    assert o <= o_lora2
    waste, _ = at("waste", [P, T], F32, o_lora2 + 4 * K8 * AR)
    b2raw, o = at("b2raw", [P, K8, AR], F32, o_lora2)
    p2, o_p3 = at("p2", [P, K8, T], F32, o_phase)
    p3, o_st = at("p3", [P, 2, K8, T], F32R, o_p3)
    staged, o = [], o_st
    for i in range(2):
        t, o = at(f"staged{i}", [P, 2, K8, P], F32R, o)
        staged.append(t)
    o_staged_end = o
    a3raw, o = at("a3raw", [P, K8, LR], F32, o)
    b3_raw, o_part = at("b3_raw", [P, K8, R3], F32, o)
    part, o_grid = at("part", [P, 4, C], F32, o_part)
    grid, o = at("grid", [P, 2, G], F32, o_grid)
    phase, o = at("phase", [P, 6], F32, o)
    last, o = at("last", [G, 1], F32, o)
    dcol, o = at("dcol", [G, C], F32, o)
    bias_col, o = at("bias_col", [P, K8], F32, o)
    bias_p3, o = at("bias_p3", [P, K8], F32, o)
    lora_a_raw, o = at("lora_a_raw", [P, AR // P, T], F32, o_phase)
    b2_out, o = at("b2_out", [P, 2, T], F32R, o)
    c_out = []
    for i in range(AR // P + 1):
        t, o = at(f"c_out{i}", [P, LR], F32, o)
        c_out.append(t)
    hmask, o = at("hmask", [P, 2 * R2], F32, o)
    hm, o = at("hm", [KS, P], F32, o)
    hc, hs, hrow = [], [], []
    for name, two, shape, dtype in (("hrow", hrow, [P, P], F32), ("hc", hc, [KC, P], F32), ("hs", hs, [2 * KS, 2, P], F32R)):
        for i in range(2):
            t, o = at(f"{name}{i}", shape, dtype, o)
            two.append(t)
    assert o <= o_p3
    stack, o_stacks = [], o_phase
    for i in range(2):
        t, o_stacks = at(f"stack{i}", [2 * KS, 2, T], F32R, o_stacks)
        stack.append(t)
    bias_parts, _ = at("bias_parts", [1, 2, T], F32R, o_stacks)

    o = o_dense1
    def nat(name, cols, dtype=F32, parts=C):
        nonlocal o
        t, o = at(name, [parts, cols], dtype, o)
        return t
    logs, exps = nat("logs", N + 1), nat("exps", N + 1)
    e_k, e_f, e_q, e_2k = (nat(f"e_{n}", N + 1) for n in "kfqs")
    e_i = nat("e_i", N + 1, I32)
    aim, cri = nat("aim", N), nat("cri", 2 * N)
    decay, angle, em1, turns, frac, sin1, sinh, cosm1, zr, zi, den, nr, ni, tmp, tmp2 = (
        nat(f"n_{n}", N) for n in range(15))
    par = nat("par", 4 * 2 * N)
    lens_i, lens = nat("lens_i", 1, I32, P), nat("lens", 1, parts=P)
    bias8 = nat("bias8", P, parts=K8)
    zero = nat("zero", P)
    assert o <= o_fac_w
    toep_raw0, o = at("toep_raw0", [P, TOEP + TFOLD], F32, o_staged_end)
    assert o <= o_part
    xt0, _ = at("xt0", [P, T], F32, o_st + 4 * T)
    toep_raw, xt = [toep_raw0], [xt0]
    ut, dt, toep, utf, tri = [], [], [], [], []
    o = o_p3
    for name, to, count, shape, dtype in (
            ("ut", ut, 2, [P, 2, K8, P], F32R),
            ("dt", dt, 2, [P, 2, 2, P], F32R),
            ("utf", utf, 2, [P, 3, P], F32),
            ("toep", toep, 2, [P, 2, TOEP + TFOLD], F32R),
            ("tri", tri, 2, [P, P], F32),
            ("toep_raw", toep_raw, 1, [P, TOEP + TFOLD], F32), ("xt", xt, 3, [P, T], F32)):
        for i in range(count):
            t, o = at(f"{name}_{i}", shape, dtype, o)
            to.append(t)
    udiff, o = at("udiff", [P, 2, P], F32, o)
    shared_in, o = at("shared_in", [P, QT], F32, o)
    unfolded, o = at("unfolded", [P, HB], F32, o)
    assert o <= o_st + 4 * T

    o = o_p3
    def pair(name, shape, dtype=F32):
        nonlocal o
        two = []
        for i in range(2):
            t, o = at(f"{name}{i}", shape, dtype, o)
            two.append(t)
        return two
    x1_in = pair("x1_in", [P, T])
    x2f = pair("x2f", [P, K8, P])
    x2t = pair("x2t", [P, 2, K8, P], F32R)
    y_out = pair("y_out", [P, T])
    a_gath = pair("a_gath", [P, K8, KR])
    m_gath = pair("m_gath", [P, P])
    c_gath = pair("c_gath", [KC, KR])

    ps = [nc.alloc_psum_tensor(f"ps{i}", [P, T], F32) for i in range(4)]
    kern_d = nc.dram_tensor("kern_d", [C, T + P], F32).ap()
    x1_d = nc.dram_tensor("x1_d", [B, C, T], F32).ap()
    b2_d = nc.dram_tensor("b2_d", [A2N, R2, 2, T], F32).ap()
    c_d = nc.dram_tensor("c_d", [AR + 1, LR], F32).ap()

    def f(ap):
        return ap.bitcast(F32)

    J_W3 = 0
    J_PAR = J_W3 + K8 + 1
    J_D0 = (J_PAR - 1, J_PAR + 1, J_PAR + 2, J_PAR + 3)
    J_A3 = J_D0[-1] + 1
    J_K = J_A3 + K8
    J_D1 = J_K + 2
    J_C = J_D1 + half_t
    J_ROW = J_C + AR // P + 1
    J_B3 = J_ROW + 1
    J_B2 = J_B3 + 1
    JOBS = J_B2 + AR // P
    LA_PS = (2, 3, 1)
    LA_ACT, LA_VECTOR = (4, 5), (0, 1, 2, 3, 6, 7)

    def bank(j):
        return 1 + j % 3 if j < J_D0[0] else j % 4

    def freed(j):
        return j + 1 if j < J_PAR else j

    SMALL, LATER = 3, 7
    CONSTS = 7 + 12 + 1
    FIXED = 3 + 2 * 4 + 5

    sem = nc.alloc_semaphore
    in_small, in_later, in_bias, in_la, in_b2, in_a3, in_b3, in_mix = (
        sem(f"in_{n}") for n in ("small", "later", "bias", "la", "b2", "a3", "b3", "mix"))
    in_w3 = [sem(f"in_w3_{i}") for i in range(K8)]
    in_w2 = [sem(f"in_w2_{i}") for i in range(K8)]
    consts = sem("consts")
    chain = sem("chain")
    pchain = sem("pchain")
    base_ready = sem("base_ready")
    trig_in, trig_out = sem("trig_in"), sem("trig_out")
    part_ready = sem("part_ready")
    fac_sum, fac_mid = sem("fac_sum"), sem("fac_mid")
    la_done, la_vector, la_scalar = sem("la_done"), sem("la_vector"), sem("la_scalar")
    fac_turns, fac_decay = sem("fac_turns"), sem("fac_decay")
    fac_arg, fac_sin, fac_exp = sem("fac_arg"), sem("fac_sin"), sem("fac_exp")
    factors = sem("factors")
    w3_ready, p2_ready = sem("w3_ready"), sem("p2_ready")
    job_done, job_hi = sem("job_done"), sem("job_hi")
    job_free = sem("job_free")
    staged_hi, staged_lo = sem("staged_hi"), sem("staged_lo")
    kern_ready, kern_stored = sem("kern_ready"), sem("kern_stored")
    fixed = sem("fixed")
    stack_copied = sem("stack_copied")
    bias_ready = sem("bias_ready")
    b2_hi, b2_stored = sem("b2_hi"), sem("b2_stored")
    c_stored = sem("c_stored")

    def ready(eng, semaphore, value):
        if not isinstance(value, int) or value > 0:
            eng.wait_ge(semaphore, value)

    x_in = [sem(f"x_in{i}") for i in range(4)]
    x1_stored = [sem(f"x1_stored{i}") for i in range(4)]
    toep_in = [sem(f"toep_in{i}") for i in range(2)]
    toep_hi, toep_lo = sem("toep_hi"), sem("toep_lo")
    ut_ps, ut_hi, ut_lo = sem("ut_ps"), sem("ut_hi"), sem("ut_lo")
    diff_ready, dt_hi, dt_lo = sem("diff_ready"), sem("dt_hi"), sem("dt_lo")
    tri_ready, utf_ready = sem("tri_ready"), sem("utf_ready")
    fold_begun, folded = sem("fold_begun"), sem("folded")
    shared_out, unfold_done = sem("shared_out"), sem("unfold_done")
    conv_done, x1_ready = sem("conv_done"), sem("x1_ready")
    mask_begun = sem("mask_begun")
    GROUPS = C // 4

    def over_channels(eng, body):
        for u in range(4):
            body(0, u)
        with eng.Fori(1, GROUPS) as k:
            for u in range(4):
                body(k, u)

    toep_view = bass.AP(tensor=kern_d.tensor, offset=0, ap=[[T + P, C], [1, P], [1, T]])
    b2_rows = b2_d.rearrange("a r h t -> (a r) h t")
    STAGES = [p2[:, :, i * P:(i + 1) * P] for i in range(K8)] + [b2raw[:, :, i * P:(i + 1) * P] for i in range(AR // P)]
    STAGE_JOBS = list(J_D0) + list(range(J_D1, J_D1 + half_t)) + list(range(J_B2, J_B2 + AR // P))

    with nc.Block() as block:
        @block.sync
        def _(sp):
            for to, of in ((logs[:, 0:N], log_a_real), (logs[:, N:N + 1], log_dt.unsqueeze(1)), (aim[:], a_imag)):
                sp.dma_start(to, of).then_inc(in_small, 16)
            def load_p2(i):
                cols = slice(i * P, (i + 1) * P)
                sp.dma_start(p2[:, :, cols], w2.rearrange("(c p) t -> p c t", p=P)[:, :, cols]).then_inc(in_w2[i], 16)

            for i in range(K8):
                cols = slice(i * P, (i + 1) * P)
                sp.dma_start(w3_raw[:, :, cols], w3.rearrange("(c p) d -> p c d", p=P)[:, :, cols]).then_inc(in_w3[i], 16)
                if i == 1:
                    load_p2(0)
                    sp.wait_ge(consts, 7)
                    sp.dma_start(kern_d[:, T:T + P], zero[:]).then_inc(kern_stored, 16)
            for i in range(1, K8):
                load_p2(i)
            sp.dma_start(b3t[:], bias2.unsqueeze(0).to_broadcast([P, T])).then_inc(in_bias, 16)
            for c in range(K8):
                sp.dma_start(a3raw[:, c, :].rearrange("p (l r) -> p l r", r=R3),
                             lora3_a.rearrange("l (c p) r -> c p l r", p=P)[c]).then_inc(in_a3, 16)
            for c in range(K8):
                sp.dma_start(b2raw[:, c, :].rearrange("p (a r) -> p a r", r=R2),
                             lora2_b.rearrange("a (c p) r -> c p a r", p=P)[c]).then_inc(in_b2, 16)
            sp.dma_start(b3_raw[:], lora3_b.rearrange("(c p) r -> p c r", p=P)).then_inc(in_b3, 16)

            sp.wait_ge(kern_ready, 1)
            sp.dma_start(kern_d[:, 0:T].rearrange("h (q r) -> q h r", q=G), kern[:]).then_inc(kern_stored, 16)
            sp.wait_ge(job_done, J_C)
            sp.dma_start(lora_a_raw[:], lora2_a.rearrange("(c a) r t -> (a r) c t", c=AR // P)).then_inc(in_la, 16)
            for m in range(AR // P + 1):
                sp.wait_ge(job_free, freed(J_C + m))
                rows = P if m < AR // P else 1
                sp.dma_start(c_d[m * P:m * P + rows], c_out[m][0:rows]).then_inc(c_stored, 16)

            def load_x(k, u):
                if not isinstance(k, int) or k > 0:
                    sp.wait_ge(x1_stored[u], 16 * k)
                sp.dma_start(xt[u][:], x[:, bass.ds(4 * k + u, 1), :].squeeze(1)).then_inc(x_in[u], 16)

            def load_toep(k, u):
                h = 4 * k + u
                ready(sp, toep_hi, h - 1)
                ready(sp, toep_lo, h - 1)
                ready(sp, dt_lo, h - 1)
                sp.dma_start(toep_raw[u % 2][:, RAW0:], toep_view[bass.ds(h, 1), :, :].squeeze(0)).then_inc(toep_in[u % 2], 16)

            def store_x1(k, u):
                sp.wait_ge(x1_ready, 4 * k + u + 1)
                sp.dma_start(x1_d[:, bass.ds(4 * k + u, 1), :].squeeze(1), xt[u][:]).then_inc(x1_stored[u], 16)

            sp.wait_ge(kern_stored, 32)
            for half in range(2):
                sp.dma_start(mix[C * half:C * half + C], mix_w.rearrange("s c d -> c s d")).then_inc(in_mix, 16)
            sp.wait_ge(job_done, J_B3 + 1)
            load_toep(0, 0)
            for m in range(AR // P):
                if m == AR // P - 2:
                    sp.wait_ge(job_done, JOBS - 1)
                    load_x(0, 0)
                sp.wait_ge(job_free, freed(J_B2 + m))
                sp.dma_start(b2_rows[m * P:(m + 1) * P], f(b2_out[:])).then_inc(b2_stored, 16)
            sp.wait_ge(job_done, JOBS)
            for u in range(1, 3):
                load_x(0, u)
                load_toep(0, u)

            def channel(k, u, loads=True):
                if loads or u < 1:
                    load_toep(k + (u + 3) // 4, (u + 3) % 4)
                    load_x(k + (u + 3) // 4, (u + 3) % 4)
                store_x1(k, u)

            for u in range(4):
                channel(0, u)
            with sp.Fori(1, GROUPS - 1) as k:
                for u in range(4):
                    channel(k, u)
            for u in range(4):
                channel(GROUPS - 1, u, loads=False)
                if u == 2:
                    sp.wait_ge(fixed, FIXED)
                    for to, of in ((stack[1][B3_ROWS], stack[0][B3_ROWS]),
                                   (stack[1][KS + 2 * R2:2 * KS, 0], stack[0][KS + 2 * R2:2 * KS, 0]),
                                   (stack[0][KS:KS + 2, 1], bias_parts[:]), (stack[1][KS:KS + 2, 1], bias_parts[:])):
                        sp.dma_start(f(to), f(of)).then_inc(stack_copied, 16)
            sp.wait_ge(stack_copied, 16 * 4)
            for u in range(4):
                sp.wait_ge(x1_stored[u], 16 * GROUPS)
            sp.wait_ge(b2_stored, 16 * (AR // P))
            sp.wait_ge(c_stored, 16 * (AR // P + 1))

        @block.gpsimd
        def _(pool):
            made = [0]

            def const(ins):
                made[0] += 1
                ins.then_inc(consts, 1)
                pool.wait_ge(consts, made[0])

            const(nc.gpsimd.memset(ident[:], 0.0))
            const(nc.gpsimd.affine_select(ident[:], ident[:], pattern=[[-1, P]], base=0, channel_multiplier=1,
                                          compare_op=ALU.not_equal, fill=1.0))
            const(nc.gpsimd.iota(grid[:, 0, :], pattern=[[-G, G]], base=G * (G - 1), channel_multiplier=0,
                                 allow_small_or_imprecise_dtypes=True))
            const(nc.gpsimd.iota(grid[:, 1, :], pattern=[[-1, G]], base=G - 1, channel_multiplier=0,
                                 allow_small_or_imprecise_dtypes=True))
            const(nc.gpsimd.memset(last[:], 0.0))
            const(nc.gpsimd.affine_select(last[:], last[:], pattern=[[0, 1]], base=1 - G, channel_multiplier=1,
                                          compare_op=ALU.not_equal, fill=1.0))
            const(nc.gpsimd.memset(zero[:], 0.0))
            for half, turns3 in enumerate(((0.25, 0.5, 0.25), (0.5, 0.75, 0.0))):
                for j, turn in enumerate(turns3):
                    const(nc.gpsimd.memset(phase[64 * half:64 * half + 64, j:j + 1], turn))
                    const(nc.gpsimd.memset(phase[64 * half:64 * half + 64, 3 + j:4 + j], turn * TWO_PI))
            const(nc.gpsimd.iota(ramp[:], pattern=[[1, T]], base=0, channel_multiplier=0,
                                 allow_small_or_imprecise_dtypes=True))
            assert made[0] == CONSTS

            steps_done = [0]

            def link(ins):
                steps_done[0] += 1
                ins.then_inc(pchain, 1)
                pool.wait_ge(pchain, steps_done[0])

            tt = nc.gpsimd.tensor_tensor

            def stage_low(n):
                pool.wait_ge(staged_hi, n + 1)
                tt(staged[n % 2][:, 1], STAGES[n], f(staged[n % 2][:, 0]), ALU.subtract).then_inc(staged_lo, 1)

            def add_identity(weights, landed, added, i):
                block_of = weights[:, i, i * P:(i + 1) * P]
                pool.wait_ge(landed[i], 16)
                tt(block_of, block_of, ident[:], ALU.add).then_inc(added, 1)

            for i in range(K8):
                add_identity(w3_raw, in_w3, w3_ready, i)
                if i == 1:
                    add_identity(p2, in_w2, p2_ready, 0)
                if i == 2:
                    stage_low(0)
            for i in range(1, K8):
                add_identity(p2, in_w2, p2_ready, i)
                if i in (2, 5):
                    stage_low(1 + i // 5)

            def across(j):
                return part[:, j, :].unsqueeze(2).to_broadcast([P, C, G])

            def steps_of(j):
                return grid[:, j, :].unsqueeze(1).to_broadcast([P, C, G])

            pool.wait_ge(part_ready, 1)
            pool.wait_ge(kern_stored, 16)
            tt(fac_v[:], across(1), steps_of(0), ALU.mult).then_inc(fac_turns, 1)
            stage_low(3)
            tt(fac_t[:], across(0), steps_of(0), ALU.mult).then_inc(fac_decay, 1)
            pool.wait_ge(fac_exp, 1)
            pool.wait_ge(fac_sin, 1)
            link(tt(fac_u[:], fac_u[:], fac_t[:], ALU.mult))
            tt(fac_u[:], fac_u[:], across(2), ALU.mult).then_inc(fac_sum, 1)
            pool.wait_ge(fac_arg, 2)
            tt(fac_v[:], across(1), steps_of(1), ALU.mult).then_inc(fac_turns, 1)
            pool.wait_ge(fac_mid, 1)
            tt(fac_t[:], across(0), steps_of(1), ALU.mult).then_inc(fac_decay, 1)

            for n in range(4, len(STAGES)):
                if n == K8:
                    pool.wait_ge(in_b2, 16 * K8)
                stage_low(n)

            def toep_low(k, u):
                h = 4 * k + u
                pool.wait_ge(toep_hi, h + 1)
                nc.gpsimd.tensor_tensor(toep[u % 2][:, 1, 0:T], toep_raw[u % 2][:, :RAW0 - 1:-1], f(toep[u % 2][:, 0, 0:T]),
                                        ALU.subtract).then_inc(toep_lo, 1)

            def fold(k, u):
                k, u = k + u // 4, u % 4
                pool.wait_ge(toep_in[u % 2], 32 * k + 16 * (u // 2) + 16)
                raw = toep_raw[u % 2]
                tt(raw[:, 0:RAW0], raw[:, RAW0:2 * RAW0], raw[:, RAW0 + QT:2 * RAW0 + QT], ALU.add).then_inc(fold_begun, 1)
                pool.wait_ge(fold_begun, 4 * k + u + 1)
                tt(raw[:, RAW0:TFOLD], raw[:, 2 * RAW0:RAW0 + TFOLD], raw[:, 2 * RAW0 + QT:RAW0 + TFOLD + QT], ALU.add).then_inc(folded, 1)

            def channel(k, u, ahead=True):
                toep_low(k, u)
                if ahead:
                    fold(k, u + 1)

            fold(0, 0)
            for u in range(4):
                channel(0, u)
            with pool.Fori(1, GROUPS - 1) as k:
                for u in range(4):
                    channel(k, u)
            for u in range(4):
                channel(GROUPS - 1, u, ahead=u < 3)

            pool.wait_ge(in_mix, 32)
            pool.wait_ge(toep_lo, C)
            for half in range(2):
                rows = slice(C * half, C * half + C)
                link(tt(mix[rows], mix[rows], ident[rows, C * half:C * half + C].unsqueeze(1).to_broadcast([C, S1, C]), ALU.add))

        @block.scalar
        def _(act):
            def trig(to, scale, bias):
                nc.scalar.activation(to, to, ACT.Sin, scale=scale, bias=bias).then_inc(fac_sin, 1)

            for to, of in ((cri[:], ssm_c.rearrange("h n c -> h (n c)")), (lens_i[:], steps.unsqueeze(1)),
                           (dcol[:], ssm_d.unsqueeze(0).to_broadcast([G, C])),
                           (bias8[:], bias2.rearrange("(c p) -> c p", p=P)),
                           (index[:, 0:B], cond.unsqueeze(0)), (index[:, B:2 * B], adapter.unsqueeze(0)),
                           (index[:, 2 * B:3 * B], labeler.unsqueeze(0))):
                act.dma_start(to, of).then_inc(in_later, 16)

            def high(j, to, of):
                act.wait_ge(job_done, j + 1)
                nc.scalar.activation(to, of, ACT.Copy).then_inc(job_hi, 1)

            def stage_high(n):
                if n < K8:
                    act.wait_ge(p2_ready, n + 1)
                elif n == K8:
                    act.wait_ge(in_b2, 16 * K8)
                if n >= 2:
                    act.wait_ge(job_done, STAGE_JOBS[n - 2] + 1)
                nc.scalar.activation(staged[n % 2][:, 0], STAGES[n], ACT.Copy).then_inc(staged_hi, 1)

            for i in range(K8):
                high(J_W3 + i, p3[:, 0, i, :], ps[bank(J_W3 + i)][:])
                if i == 0:
                    act.wait_ge(trig_in, 1)
                    nc.scalar.activation(sin1[:], frac[:], ACT.Sin, scale=TWO_PI).then_inc(trig_out, 1)
                    nc.scalar.activation(sinh[:], frac[:], ACT.Sin, scale=TWO_PI / 2).then_inc(trig_out, 1)
                if i == 1:
                    stage_high(0)
            stage_high(1)
            stage_high(2)

            def dense0_high(i):
                high(J_D0[i], dense0[:, 0, i, 0:T], ps[J_D0[i] % 4][:])

            stage_high(3)
            act.wait_ge(bias_ready, 1)
            dense0_high(0)
            dense0_high(1)
            act.wait_ge(fac_decay, 1)
            nc.scalar.activation(fac_t[:], fac_t[:], ACT.Exp).then_inc(fac_exp, 1)
            act.wait_ge(fac_arg, 1)
            trig(fac_u[:], -TWO_PI, phase[:, 3:4])
            act.wait_ge(fac_arg, 2)
            trig(fac_w[:], -TWO_PI, phase[:, 4:5])
            dense0_high(2)
            stage_high(4)
            dense0_high(3)
            stage_high(5)
            act.wait_ge(fac_decay, 2)
            nc.scalar.activation(fac_t[:], fac_t[:], ACT.Exp).then_inc(fac_exp, 1)
            act.wait_ge(fac_arg, 3)
            trig(fac_w[:], -TWO_PI, phase[:, 5:6])
            act.wait_ge(kern_stored, 32)
            for i in range(half_t):
                stage_high(half_t + i + 2)
                high(J_D1 + i, dense1[:, 0, i, 0:T], ps[(J_D1 + i) % 4][:])
            for m in range(AR // P):
                act.wait_ge(job_done, J_B2 + m + 1)
                if m >= 1:
                    act.wait_ge(b2_stored, 16 * m)
                nc.scalar.activation(b2_out[:, 0], ps[(J_B2 + m) % 4][:], ACT.Copy).then_inc(b2_hi, 1)
                if m + K8 + 2 < len(STAGES):
                    stage_high(m + K8 + 2)

            def split_high(k, u):
                h = 4 * k + u
                act.wait_ge(folded, h + 1)
                ready(act, conv_done, h - 1)
                nc.scalar.activation(tri[u % 2][:], toep_raw[u % 2][:, :TOEP + TFOLD - P - 1:-1], ACT.Copy).then_inc(tri_ready, 1)
                nc.scalar.activation(toep[u % 2][:, 0], toep_raw[u % 2][:, ::-1], ACT.Copy).then_inc(toep_hi, 1)
                act.wait_ge(ut_ps, h + 1)
                xp = ps[0][:].rearrange("p (i b) -> p i b", i=K8)
                nc.scalar.activation(utf[u % 2][:, 0:2], xp[:, 2:4], ACT.Copy)
                nc.scalar.activation(ut[u % 2][:, 0], xp, ACT.Copy).then_inc(ut_hi, 1)
                nc.scalar.activation(utf[u % 2][:, 2], xp[:, K8 - 1], ACT.Copy).then_inc(utf_ready, 1)
                if isinstance(h, int) and h == 0:
                    for i in LA_ACT:
                        act.wait_ge(la_done, i + 1)
                        nc.scalar.activation(lora2_in[:, i, :], ps[LA_PS[i % 3]][:, 0:AR], ACT.Copy).then_inc(la_scalar, 1)
                act.wait_ge(diff_ready, h + 1)
                nc.scalar.activation(dt[u % 2][:, 0], udiff[:], ACT.Copy).then_inc(dt_hi, 1)

            act.wait_ge(job_done, JOBS)
            over_channels(act, split_high)

        @block.vector
        def _(dve):
            count = [0]

            def link(ins):
                count[0] += 1
                ins.then_inc(chain, 1)
                dve.wait_ge(chain, count[0])

            tt, ts, stt = nc.vector.tensor_tensor, nc.vector.tensor_scalar, nc.vector.scalar_tensor_tensor
            highs = [0]

            def low(j, to, of, high):
                highs[0] += 1
                dve.wait_ge(job_hi, highs[0])
                tt(to, of, f(high), ALU.subtract).then_inc(job_free, 1)

            def p3_low(i):
                low(J_W3 + i, p3[:, 1, i, :], ps[bank(J_W3 + i)][:], p3[:, 0, i, :])

            def exp_parts(z, k, r, q, two_k, ki):
                link(ts(k, z, LOG2E, ROUND, ALU.mult, ALU.add))
                link(ts(k, k, ROUND, -126.0, ALU.subtract, ALU.max))
                link(ts(k, k, 127.0, None, ALU.min))
                link(stt(r, k, -LN2_HI, z, ALU.mult, ALU.add))
                link(stt(r, k, -LN2_LO, r, ALU.mult, ALU.add))
                link(ts(q, r, 1.0 / 40320, None, ALU.mult))
                for n in (5040, 720, 120, 24, 6, 2, 1):
                    link(stt(q, q, 1.0 / n, r, ALU.add, ALU.mult))
                link(ts(ki, k, 127.0, None, ALU.add))
                link(ts(two_k.bitcast(I32), ki, 23, None, ALU.logical_shift_left))

            dve.wait_ge(in_small, 16 * SMALL)
            exp_parts(logs[:], e_k[:], e_f[:], e_q[:], e_2k[:], e_i[:])
            link(tt(e_q[:], e_q[:], e_2k[:], ALU.mult))
            link(tt(exps[:], e_q[:], e_2k[:], ALU.add))
            ar, step_time = exps[:, 0:N], exps[:, N:N + 1]
            link(ts(decay[:], ar, step_time, -1.0, ALU.mult, ALU.mult))
            link(ts(angle[:], aim[:], step_time, None, ALU.mult))
            link(ts(turns[:], angle[:], 1.0 / (2 * math.pi), None, ALU.mult))
            link(ts(tmp[:], turns[:], ROUND, ROUND, ALU.add, ALU.subtract))
            dve.wait_ge(chain, count[0])
            tt(frac[:], turns[:], tmp[:], ALU.subtract).then_inc(trig_in, 1)
            p3_low(0)
            p3_low(1)
            exp_parts(decay[:], e_k[:, 0:N], e_f[:, 0:N], e_q[:, 0:N], e_2k[:, 0:N], e_i[:, 0:N])
            link(tt(e_q[:, 0:N], e_q[:, 0:N], e_2k[:, 0:N], ALU.mult))
            link(ts(e_f[:, 0:N], e_2k[:, 0:N], 1.0, None, ALU.subtract))
            link(tt(em1[:], e_q[:, 0:N], e_f[:, 0:N], ALU.add))
            p3_low(2)
            p3_low(3)
            p3_low(4)
            dve.wait_ge(trig_out, 2)
            link(tt(tmp[:], sinh[:], sinh[:], ALU.mult))
            link(ts(cosm1[:], tmp[:], -2.0, None, ALU.mult))
            link(stt(zr[:], cosm1[:], 1.0, em1[:], ALU.add, ALU.mult))
            link(tt(zr[:], zr[:], cosm1[:], ALU.add))
            link(stt(zi[:], em1[:], 1.0, sin1[:], ALU.add, ALU.mult))
            p3_low(5)
            p3_low(6)
            p3_low(7)
            link(tt(tmp[:], ar, ar, ALU.mult))
            link(tt(den[:], aim[:], aim[:], ALU.mult))
            link(tt(den[:], den[:], tmp[:], ALU.add))
            link(nc.vector.reciprocal(den[:], den[:]))
            link(tt(nr[:], zi[:], aim[:], ALU.mult))
            link(tt(tmp[:], zr[:], ar, ALU.mult))
            link(tt(nr[:], nr[:], tmp[:], ALU.subtract))
            link(stt(nr[:], nr[:], 2.0, den[:], ALU.mult, ALU.mult))
            link(tt(ni[:], zr[:], aim[:], ALU.mult))
            link(tt(tmp[:], zi[:], ar, ALU.mult))
            link(tt(ni[:], ni[:], tmp[:], ALU.add))
            link(stt(ni[:], ni[:], -2.0, den[:], ALU.mult, ALU.mult))
            dve.wait_ge(in_later, 16 * LATER)
            c3 = cri[:].rearrange("h (n c) -> h n c", c=2)
            p4 = par[:].rearrange("h (j d n) -> h j d n", j=4, d=2)
            def both(j):
                return p4[:, j, :, :]
            def twice(t):
                return t[:].unsqueeze(1).to_broadcast([C, 2, N])
            link(nc.vector.tensor_copy(both(0), twice(decay)))
            link(nc.vector.tensor_copy(both(1), twice(turns)))
            link(tt(tmp[:], nr[:], c3[:, :, 0], ALU.mult))
            link(tt(tmp2[:], ni[:], c3[:, :, 1], ALU.mult))
            link(tt(both(2), twice(tmp), twice(tmp2), ALU.subtract))
            link(tt(tmp[:], nr[:], c3[:, :, 1], ALU.mult))
            link(tt(tmp2[:], ni[:], c3[:, :, 0], ALU.mult))
            link(tt(both(3), twice(tmp), twice(tmp2), ALU.add))
            nc.vector.tensor_copy(lens[:], lens_i[:]).then_inc(base_ready, 1)
            dve.wait_ge(base_ready, 1)
            dve.wait_ge(consts, CONSTS)
            link(ts(mask[:], ramp[:], lens[:], None, ALU.is_lt))
            mask_made = count[0]

            def bias_products(first, end):
                for c in range(first, end):
                    link(nc.vector.tensor_tensor_reduce(out=waste[:], in0=w3_raw[:, c, :], in1=b3t[:], scale=1.0, scalar=0.0,
                                                        op0=ALU.mult, op1=ALU.add, accum_out=bias_p3[:, c:c + 1]))

            dve.wait_ge(in_bias, 16)
            dve.wait_ge(w3_ready, K8)
            bias_products(0, 2)
            dve.wait_ge(job_done, J_PAR + 1)
            link(nc.vector.tensor_copy(part[:], ps[J_PAR % 4][:, 0:4 * C].rearrange("p (j h) -> p j h", j=4)))
            nc.vector.tensor_copy(bias_col[:], ps[J_PAR % 4][:, 4 * C:4 * C + K8]).then_inc(part_ready, 1)

            def reduced(to, of, j):
                link(ts(to, of, phase[:, j:j + 1], ROUND, ALU.add, ALU.add))
                stt(to, to, ROUND, of, ALU.subtract, ALU.subtract).then_inc(fac_arg, 1)

            bias_products(2, 5)
            dve.wait_ge(fac_turns, 1)
            reduced(fac_u[:], fac_v[:], 0)
            bias_products(5, K8)
            nc.vector.memset(waste[:, 0:1], 0.0).then_inc(bias_ready, 1)

            def dense0_low(i):
                low(J_D0[i], dense0[:, 1, i, 0:T], ps[J_D0[i] % 4][:], dense0[:, 0, i, 0:T])

            dense0_low(0)
            reduced(fac_w[:], fac_v[:], 1)
            dense0_low(1)
            def across(j):
                return part[:, j, :].unsqueeze(2).to_broadcast([P, C, G])

            dve.wait_ge(part_ready, 1)
            dve.wait_ge(fac_exp, 1)
            dve.wait_ge(fac_sin, 2)
            tt(fac_w[:], fac_w[:], fac_t[:], ALU.mult).then_inc(fac_mid, 1)
            dve.wait_ge(fac_mid, 1)
            link(tt(fac_w[:], fac_w[:], across(3), ALU.mult))
            dve.wait_ge(fac_sum, 1)
            link(tt(fac_u[:], fac_u[:], fac_w[:], ALU.add))
            dense0_low(2)
            dense0_low(3)

            def copied(j, to, of, scale=None):
                dve.wait_ge(job_done, j + 1)
                if scale is None:
                    return nc.vector.tensor_copy(to, of)
                return ts(to, of, scale, None, ALU.mult)

            for i in range(K8):
                copied(J_A3 + i, lora3_in[:, i, :], ps[(J_A3 + i) % 4][:, 0:LR]).then_inc(job_free, 1)
                if i == 0:
                    dve.wait_ge(fac_turns, 2)
                    reduced(fac_w[:], fac_v[:], 2)
                if i == 3:
                    dve.wait_ge(fac_exp, 2)
                    dve.wait_ge(fac_sin, 3)
                    tt(fac_v[:], fac_w[:], fac_t[:], ALU.mult).then_inc(factors, 1)
            for i in range(2):
                j = J_K + i
                dve.wait_ge(job_done, j + 1)
                nc.vector.tensor_copy(kern[:, i * C // 2:(i + 1) * C // 2, :],
                                      ps[j % 4][0:G, :].rearrange("q (h r) -> q h r", r=G)).then_inc(job_free, 1)
            dve.wait_ge(job_free, freed(J_K + 1))
            link(ts(dcol[:], dcol[:], 1.0, last[:], ALU.add, ALU.mult))
            tt(kern[:, :, G - 1], kern[:, :, G - 1], dcol[:], ALU.add).then_inc(kern_ready, 1)
            for i in range(half_t):
                low(J_D1 + i, dense1[:, 1, i, 0:T], ps[(J_D1 + i) % 4][:], dense1[:, 0, i, 0:T])

            for m in range(AR // P + 1):
                rows = P if m < AR // P else 1
                copied(J_C + m, c_out[m][0:rows], ps[(J_C + m) % 4][0:rows, 0:LR]).then_inc(job_free, 1)
            copied(J_ROW, b3t[0:1], ps[J_ROW % 4][0:1, :]).then_inc(job_free, 1)
            copied(J_B3, b3t[B3_ROWS], ps[J_B3 % 4][0:R3, :], 0.5).then_inc(job_free, 1)

            made = [0]

            def fix(ins):
                made[0] += 1
                ins.then_inc(fixed, 1)
                dve.wait_ge(fixed, made[0])

            fix(nc.vector.memset(hmask[:], 0.0))
            for b in range(2):
                fix(nc.vector.memset(hmask[b * C:(b + 1) * C, b * R2:(b + 1) * R2], 1.0))
            for v in range(2):
                fix(nc.vector.memset(hrow[v][:], 0.0))
                for b in range(2):
                    fix(nc.vector.tensor_copy(hc[v][2 * R2:KC, b * C:(b + 1) * C],
                                              ident[2 * R2:KC, 2 * R2 + b:2 * R2 + b + 1].to_broadcast([2, C])))
                fix(nc.vector.memset(f(hs[v][KS:KS + 2, 1]), 1.0))

            for m in range(AR // P):
                dve.wait_ge(b2_hi, m + 1)
                tt(b2_out[:, 1], ps[(J_B2 + m) % 4][:], f(b2_out[:, 0]), ALU.subtract).then_inc(job_free, 1)
            def a2_copied(i):
                dve.wait_ge(la_done, i + 1)
                nc.vector.tensor_copy(lora2_in[:, i, :], ps[LA_PS[i % 3]][:, 0:AR]).then_inc(la_vector, 1)

            def transposed_low(k, u):
                h = 4 * k + u
                dve.wait_ge(utf_ready, h + 1)
                tt(ut[u % 2][:, 1], ps[0][:].rearrange("p (i b) -> p i b", i=K8), f(ut[u % 2][:, 0]),
                   ALU.subtract).then_inc(ut_lo, 1)
                dve.wait_ge(toep_hi, h + 1)
                tt(toep[u % 2][:, 1, T:], toep_raw[u % 2][:, RAW0 - 1::-1], f(toep[u % 2][:, 0, T:]), ALU.subtract)
                ready(dve, dt_lo, h)
                tt(udiff[:], ps[0][:, 0:QT].rearrange("p (i b) -> p i b", i=2), utf[u % 2][:, 0:2], ALU.subtract).then_inc(diff_ready, 1)
                dve.wait_ge(dt_hi, h + 1)
                tt(dt[u % 2][:, 1], udiff[:], f(dt[u % 2][:, 0]), ALU.subtract).then_inc(dt_lo, 1)

            def masked(k, u):
                h = 4 * k + u
                y, shared = ps[2 + u % 2], ps[1][:, (u % 2) * HB:(u % 2) * HB + QT]
                dve.wait_ge(conv_done, h + 1)
                ready(dve, unfold_done, h)
                nc.vector.tensor_copy(shared_in[:], shared).then_inc(shared_out, 1)
                dve.wait_ge(chain, mask_made)
                nc.vector.copy_predicated(xt[u][:, 0:HB], mask[:, 0:HB], y[:, 0:HB])
                dve.wait_ge(shared_out, h + 1)
                ready(dve, x1_ready, h)
                tt(unfolded[:, 0:QT], y[:, HB:HB + QT], shared_in[:], ALU.add)
                tt(unfolded[:, QT:HB], y[:, HB + QT:T], shared_in[:], ALU.subtract).then_inc(unfold_done, 1)
                dve.wait_ge(unfold_done, h + 1)
                dve.sem_inc(mask_begun, 1)
                nc.vector.copy_predicated(xt[u][:, HB:T], mask[:, HB:T], unfolded[:]).then_inc(x1_ready, 1)

            def channel(k, u, ahead=True):
                if ahead:
                    transposed_low(k + (u + 1) // 4, (u + 1) % 4)
                masked(k, u)

            for i in (0, 1, 2, 3):
                a2_copied(i)
            transposed_low(0, 0)
            for i in (6, 7):
                a2_copied(i)
            for u in range(4):
                channel(0, u)
            with dve.Fori(1, GROUPS - 1) as k:
                for u in range(4):
                    channel(k, u)
            dve.wait_ge(b2_stored, 16 * (AR // P))
            constant = (((stack[0][B3_ROWS, 0], b3t[B3_ROWS], None), (stack[0][B3_ROWS, 1], b3t[B3_ROWS], stack[0][B3_ROWS, 0])),
                        ((stack[0][KS + 2 * R2:2 * KS, 0], b3t[B3_ROWS], None),),
                        ((bias_parts[:, 0], b3t[0:1], None), (bias_parts[:, 1], b3t[0:1], bias_parts[:, 0])))
            for u in range(4):
                channel(GROUPS - 1, u, ahead=u < 3)
                if u < 3:
                    for to, of, high in constant[u]:
                        fix(nc.vector.tensor_copy(to, of) if high is None else tt(to, of, f(high), ALU.subtract))
            assert made[0] == FIXED

        @block.tensor
        def _(pe):
            mm = nc.tensor.matmul
            PASSES = ((0, 0), (0, 1), (1, 0))

            def job(j):
                if j < J_D0[0]:
                    if j >= 3:
                        pe.wait_ge(job_free, freed(j - 3))
                elif j < J_D0[0] + 4:
                    pass
                elif j - 4 == J_PAR:
                    pe.wait_ge(part_ready, 1)
                else:
                    pe.wait_ge(job_free, freed(j - 4))
                return ps[bank(j)]

            def over_chunks(out_ap, lhs, rhs):
                for i in range(K8):
                    ins = mm(out_ap, lhs(i), rhs(i), start=i == 0, stop=i == K8 - 1)
                return ins

            stages = [0]

            def split_job(j, between=None):
                n = stages[0]
                stages[0] += 1
                t = job(j)
                pe.wait_ge(staged_lo, n + 1)
                for half in range(2):
                    cols = slice(half * HB, (half + 1) * HB)
                    for c in range(K8):
                        for a, b in PASSES:
                            ins = mm(t[:, cols], staged[n % 2][:, a, c, :], p3[:, b, c, cols],
                                     start=c == a == b == 0, stop=c == K8 - 1 and a == 1)
                    if half == 0 and between is not None:
                        between()
                ins.then_inc(job_done, 1)

            def transpose_w3(i):
                t = job(J_W3 + i)
                pe.wait_ge(w3_ready, i + 1)
                for c in range(K8):
                    ins = nc.tensor.transpose(t[:, c * P:(c + 1) * P], w3_raw[:, c, i * P:(i + 1) * P], ident[:])
                ins.then_inc(job_done, 1)

            first_out = job(J_D0[0])
            stages[0] += 1
            for i in range(3):
                transpose_w3(i)
            for c in range(K8):
                if c + 3 < K8:
                    transpose_w3(c + 3)
                pe.wait_ge(job_free, freed(J_W3 + c))
                pe.wait_ge(staged_lo, 1)
                for half in range(2):
                    cols = slice(half * HB, (half + 1) * HB)
                    for a, b in PASSES:
                        ins = mm(first_out[:, cols], staged[0][:, a, c, :], p3[:, b, c, cols],
                                 start=c == a == b == 0, stop=c == K8 - 1 and a == 1)
            ins.then_inc(job_done, 1)
            def parameters():
                t = job(J_PAR)
                pe.wait_ge(base_ready, 1)
                pe.wait_ge(in_later, 16 * LATER)
                for q in range(4):
                    nc.tensor.transpose(t[:, q * C:(q + 1) * C], par[:, q * 2 * N:(q + 1) * 2 * N], ident[0:C, 0:C])
                nc.tensor.transpose(t[:, 4 * C:4 * C + K8], bias8[:], ident[0:K8, 0:K8]).then_inc(job_done, 1)

            split_job(J_D0[1], between=parameters)
            for i in range(2, half_t):
                split_job(J_D0[i])
            pe.wait_ge(p2_ready, K8)
            pe.wait_ge(in_a3, 16 * K8)
            for i in range(K8):
                t = job(J_A3 + i)
                over_chunks(t[:, 0:LR], lambda c: p2[:, c, i * P:(i + 1) * P], lambda c: a3raw[:, c, :]).then_inc(job_done, 1)
            pe.wait_ge(factors, 1)
            for q in range(2):
                t = job(J_K + q)
                for h in range(C // 2):
                    c = q * C // 2 + h
                    ins = mm(t[0:G, h * G:(h + 1) * G], fac_u[:, c, :], fac_v[:, c, :], start=True, stop=True)
                ins.then_inc(job_done, 1)
            for i in range(half_t):
                split_job(J_D1 + i)
            pe.wait_ge(in_b2, 16 * K8)
            for m in range(AR // P):
                t = job(J_C + m)
                over_chunks(t[:, 0:LR], lambda c: b2raw[:, c, m * P:(m + 1) * P], lambda c: a3raw[:, c, :]).then_inc(job_done, 1)
            t = job(J_C + AR // P)
            over_chunks(t[0:1, 0:LR], lambda c: bias_col[:, c:c + 1], lambda c: a3raw[:, c, :]).then_inc(job_done, 1)
            t = job(J_ROW)
            pe.wait_ge(bias_ready, 1)
            for c in range(K8):
                ins = mm(t[0:1, c * P:(c + 1) * P], bias_p3[:, c:c + 1], ident[:], start=True, stop=True)
            ins.then_inc(job_done, 1)
            t = job(J_B3)
            pe.wait_ge(in_b3, 16)
            for c in range(K8):
                ins = nc.tensor.transpose(t[0:R3, c * P:(c + 1) * P], b3_raw[:, c, :], ident[:])
            ins.then_inc(job_done, 1)
            for m in range(AR // P):
                split_job(J_B2 + m)
            def transpose_x(k, u):
                h = 4 * k + u
                pe.wait_ge(x_in[u], 16 * k + 16)
                ready(pe, ut_lo, h)
                ready(pe, diff_ready, h)
                for i in range(K8):
                    ins = nc.tensor.transpose(ps[0][:, i * P:(i + 1) * P], xt[u][:, i * P:(i + 1) * P], ident[:])
                ins.then_inc(ut_ps, 1)

            def convolve(k, u):
                h = 4 * k + u
                pe.wait_ge(toep_lo, h + 1)
                pe.wait_ge(dt_lo, h + 1)
                pe.wait_ge(tri_ready, h + 1)
                ready(pe, x1_ready, h - 1)
                y, xs, ds, tp = ps[2 + u % 2], ut[u % 2], dt[u % 2], toep[u % 2]
                shared = ps[1][:, (u % 2) * HB:(u % 2) * HB + QT]
                for i in range(2):
                    for a, b in PASSES:
                        at_col = HB - i * P
                        mm(shared, ds[:, a, i, :], tp[:, b, at_col:at_col + QT],
                           start=i == a == b == 0, stop=i == a == 1)
                for half in range(2):
                    for i in range(half_t - 1):
                        for a, b in PASSES:
                            mm(y[:, half * HB + i * P:(half + 1) * HB], xs[:, a, half * half_t + i, :], tp[:, b, 0:HB - i * P],
                               start=i == a == b == 0, stop=False)
                    mm(y[:, (half + 1) * HB - P:(half + 1) * HB], utf[u % 2][:, 1 + half, :], tri[u % 2][:],
                       start=False, stop=half == 0)
                for i in range(half_t):
                    to = HB if i >= 2 else HB + QT
                    at_col = TOEP + HB - i * P - P
                    for a, b in PASSES:
                        ins = mm(y[:, to:to + QT], xs[:, a, i, :], tp[:, b, at_col:at_col + QT],
                                 start=False, stop=i == half_t - 1 and a == 1)
                ins.then_inc(conv_done, 1)

            pe.wait_ge(job_free, freed(JOBS - 2))
            assert (JOBS - 2) % 4 == 0
            transpose_x(0, 0)
            pe.wait_ge(in_la, 16)
            for i in range(K8):
                t = ps[LA_PS[i % 3]]
                if i == 2:
                    pe.wait_ge(job_free, freed(JOBS - 1))
                if i - 3 in LA_ACT:
                    pe.wait_ge(la_scalar, LA_ACT.index(i - 3) + 1)
                elif i >= 3:
                    pe.wait_ge(la_vector, LA_VECTOR.index(i - 3) + 1)
                for c in range(AR // P):
                    ins = nc.tensor.transpose(t[:, c * P:(c + 1) * P], lora_a_raw[:, c, i * P:(i + 1) * P], ident[:])
                ins.then_inc(la_done, 1)
            pe.wait_ge(la_scalar, len(LA_ACT))
            pe.wait_ge(la_vector, len(LA_VECTOR))

            def channel(k, u, ahead=True):
                if ahead:
                    transpose_x(k + (u + 1) // 4, (u + 1) % 4)
                convolve(k, u)

            for u in range(4):
                channel(0, u)
            with pe.Fori(1, GROUPS - 1) as k:
                for u in range(4):
                    channel(k, u)
            for u in range(4):
                channel(GROUPS - 1, u, ahead=u < 3)


    x1_landed = [sem(f"x1_landed{i}") for i in range(2)]
    stack_landed = [sem(f"stack_landed{i}") for i in range(2)]
    y_stored = [sem(f"y_stored{i}") for i in range(2)]
    gathered_m, gathered_a = sem("gathered_m"), sem("gathered_a")
    x2_ps, x2_copied, x2_hi, x2_lo = (sem(f"x2_{n}") for n in ("ps", "copied", "hi", "lo"))
    h2_ps, hrow_ready = sem("h2_ps"), sem("hrow_ready")
    h_turned, h2_ready = sem("h_turned"), sem("h2_ready")
    h_ps, h_sum, h_hi, h_lo = sem("h_ps"), sem("h_sum"), sem("h_hi"), sem("h_lo")
    c_landed = [sem(f"c_landed{i}") for i in range(2)]
    c_zeroed = sem("c_zeroed")
    y_ps, y_left, y_right = sem("y_ps"), sem("y_left"), sem("y_right")
    a_hi, a_lo = sem("a_hi"), sem("a_lo")
    tail_out = sem("tail_out")
    gfixed = sem("gfixed")
    PAIRS = TILES // 2
    c_adapters = c_d[0:AR].rearrange("(a r) c -> a r c", r=R2)
    x1_rows = x1_d.rearrange("(n b) c t -> n (b c) t", b=2)
    out_rows = out.rearrange("(n b) c t -> n (b c) t", b=2)

    def over_tiles(eng, body):
        for v in range(2):
            body(0, v)
        with eng.Fori(1, PAIRS - 1) as k:
            for v in range(2):
                body(k, v)
        for v in range(2):
            body(PAIRS - 1, v)

    def a_parts(v):
        return [(a_gath[v][:, i * half_t:(i + 1) * half_t], w[:, :, :, T:WT]) for i, w in enumerate((dense0, dense1))]

    def exists(k, v):
        return not isinstance(k, int) or 2 * k + v < TILES

    with nc.Block() as block:
        @block.sync
        def _(sp):
            def load_x1(k, v):
                k, v = k + v // 2, v % 2
                n = 2 * k + v
                ready(sp, x2_ps, n - 1)
                sp.dma_start(x1_in[v][:], x1_rows[bass.ds(n, 1)].squeeze(0)).then_inc(x1_landed[v], 16)

            def load_stack(k, v):
                k, v = k + v // 2, v % 2
                n = 2 * k + v
                ready(sp, y_ps, n - 1)
                for b in range(2):
                    a = sp.value_load(index[0:1, bass.ds(2 * n + b + B, 1)], min_val=0, max_val=A2N - 1)
                    l = sp.value_load(index[0:1, bass.ds(2 * n + b + 2 * B, 1)], min_val=0, max_val=L3N - 1)
                    rows = slice(b * R2, (b + 1) * R2)
                    cols = slice(2 * R2, KS)
                    sp.dma_start(f(stack[v][rows]), b2_d[bass.ds(a, 1)].squeeze(0)).then_inc(stack_landed[v], 16)
                    sp.dma_start(f(stack[v][KS + b * R2:KS + (b + 1) * R2, 0]),
                                 b2_d[bass.ds(a, 1), :, 0, :].squeeze(0)).then_inc(stack_landed[v], 16)
                    sp.dma_start(c_gath[v][rows, cols], c_adapters[bass.ds(a, 1), :, bass.ds(l * R3, R3)].squeeze(0)).then_inc(c_landed[v], 16)
                    sp.dma_start(c_gath[v][2 * R2 + b:2 * R2 + b + 1, cols], c_d[AR:AR + 1, bass.ds(l * R3, R3)]).then_inc(c_landed[v], 16)

            def tile(k, v):
                if exists(k, v + 2):
                    load_x1(k, v + 2)
                n = 2 * k + v
                sp.wait_ge(y_left, n + 1)
                sp.wait_ge(y_right, n + 1)
                sp.dma_start(out_rows[bass.ds(n, 1)].squeeze(0), y_out[v][:]).then_inc(y_stored[v], 16)
                if exists(k, v + 2):
                    load_stack(k, v + 2)

            for v in range(2):
                load_x1(0, v)
            sp.wait_ge(c_zeroed, 2)
            for v in range(2):
                load_stack(0, v)
            over_tiles(sp, tile)
            for v in range(2):
                sp.wait_ge(y_stored[v], 16 * PAIRS)

        @block.gpsimd
        def _(pool):
            for v in range(2):
                nc.gpsimd.memset(m_gath[v][:], 0.0).then_inc(gfixed, 1)
            for v in range(2):
                nc.gpsimd.memset(c_gath[v][:], 0.0).then_inc(c_zeroed, 1)
            pool.wait_ge(gfixed, 2)
            pool.wait_ge(c_zeroed, 2)

            def gather(k, v):
                k, v = k + v // 2, v % 2
                n = 2 * k + v
                ready(pool, x2_ps, n - 1)
                for b in range(2):
                    s = pool.value_load(index[0:1, bass.ds(2 * n + b, 1)], min_val=0, max_val=S1 - 1)
                    rows = slice(b * C, (b + 1) * C)
                    ins = nc.gpsimd.tensor_copy(m_gath[v][rows, b * C:(b + 1) * C], mix[rows, bass.ds(s, 1), :].squeeze(1))
                ins.then_inc(gathered_m, 1)
                pool.wait_ge(gathered_m, n + 1)
                ready(pool, a_lo, n - 1)
                for b in range(2):
                    a = pool.value_load(index[0:1, bass.ds(2 * n + b + B, 1)], min_val=0, max_val=A2N - 1)
                    l = pool.value_load(index[0:1, bass.ds(2 * n + b + 2 * B, 1)], min_val=0, max_val=L3N - 1)
                    nc.gpsimd.tensor_copy(a_gath[v][:, :, b * R2:(b + 1) * R2], lora2_in[:, :, bass.ds(a * R2, R2)])
                    c = 2 * R2 + b * R3
                    ins = nc.gpsimd.tensor_copy(a_gath[v][:, :, c:c + R3], lora3_in[:, :, bass.ds(l * R3, R3)])
                ins.then_inc(gathered_a, 1)
                pool.wait_ge(gathered_a, n + 1)

            def place_low(k, v):
                k, v = k + v // 2, v % 2
                n = 2 * k + v
                pool.wait_ge(a_hi, n + 1)
                for of, to in a_parts(v):
                    ins = nc.gpsimd.tensor_tensor(to[:, 1], of, f(to[:, 0]), ALU.subtract)
                ins.then_inc(a_lo, 1)
                pool.wait_ge(a_lo, n + 1)

            gather(0, 0)
            place_low(0, 0)
            gather(0, 1)

            def tile(k, v):
                if exists(k, v + 1):
                    place_low(k, v + 1)
                if exists(k, v + 2):
                    gather(k, v + 2)

            over_tiles(pool, tile)

        @block.scalar
        def _(act):
            def x2_high(k, v):
                k, v = k + v // 2, v % 2
                n = 2 * k + v
                act.wait_ge(x2_copied, n + 1)
                ready(act, y_ps, n - 1)
                nc.scalar.activation(x2t[v][:, 0], x2f[v][:], ACT.Copy).then_inc(x2_hi, 1)

            def place_high(k, v):
                k, v = k + v // 2, v % 2
                n = 2 * k + v
                ready(act, h2_ps, n)
                act.wait_ge(gathered_a, n + 1)
                for of, to in a_parts(v):
                    ins = nc.scalar.activation(to[:, 0], of, ACT.Copy)
                ins.then_inc(a_hi, 1)

            def tile(k, v):
                if exists(k, v + 1):
                    x2_high(k, v + 1)
                    place_high(k, v + 1)
                n = 2 * k + v
                act.wait_ge(hrow_ready, n + 1)
                if not isinstance(k, int) or k > 0:
                    act.wait_ge(y_stored[v], 16 * k)
                nc.scalar.activation(y_out[v][:, T - TAIL:T], ps[3][:, 0:TAIL], ACT.Copy).then_inc(tail_out, 1)
                act.wait_ge(y_ps, n + 1)
                first, end = GROUPS_OF[0]
                nc.scalar.activation(y_out[v][:, first:end], ps[2][:, 0:end - first], ACT.Copy).then_inc(y_left, 1)

            place_high(0, 0)
            x2_high(0, 0)
            over_tiles(act, tile)

        @block.vector
        def _(dve):
            tt = nc.vector.tensor_tensor
            def x2_copy(k, v):
                k, v = k + v // 2, v % 2
                n = 2 * k + v
                dve.wait_ge(x2_ps, n + 1)
                ready(dve, x2_lo, n - 1)
                nc.vector.tensor_copy(x2f[v][:], ps[0][:].rearrange("p (i m) -> p i m", i=K8)).then_inc(x2_copied, 1)
                dve.wait_ge(x2_hi, n + 1)
                tt(x2t[v][:, 1], x2f[v][:], f(x2t[v][:, 0]), ALU.subtract).then_inc(x2_lo, 1)

            def adapter_inputs(k, v):
                n = 2 * k + v
                dve.wait_ge(h2_ps, n + 1)
                ready(dve, h_turned, n - 1)
                low = ps[3][:, TAIL:TAIL + KR]
                for b in range(2):
                    rows = slice(b * C, (b + 1) * C)
                    nc.vector.tensor_copy(hrow[v][rows, 2 * R2:KS], low[rows, 2 * R2 + b * R3:2 * R2 + (b + 1) * R3])
                tt(hrow[v][:, 0:2 * R2], low[:, 0:2 * R2], hmask[:], ALU.mult).then_inc(hrow_ready, 1)
                dve.wait_ge(h_turned, n + 1)
                ready(dve, h_ps, n - 1)
                turned = ps[1][0:KS, v * HB + P:v * HB + 2 * P]
                ready(dve, h_lo, n)
                nc.vector.tensor_copy(hm[:], turned)
                nc.vector.tensor_copy(hc[v][0:2 * R2], turned[0:2 * R2]).then_inc(h2_ready, 1)

            def low_rank(k, v):
                n = 2 * k + v
                dve.wait_ge(h_ps, n + 1)
                dve.wait_ge(h2_ready, n + 1)
                tt(hm[2 * R2:KS], hm[2 * R2:KS], ps[1][2 * R2:KS, v * HB + 2 * P:v * HB + 3 * P], ALU.add).then_inc(h_sum, 1)
                dve.wait_ge(h_sum, n + 1)
                ready(dve, y_ps, n - 1)
                nc.vector.tensor_copy(hs[v][0:KS], hm[:].unsqueeze(1).to_broadcast([KS, 2, P])).then_inc(h_hi, 1)
                dve.wait_ge(h_hi, n + 1)
                tt(hs[v][KS:2 * KS, 0], hm[:], f(hs[v][0:KS, 0]), ALU.subtract).then_inc(h_lo, 1)

            def tile(k, v):
                if exists(k, v + 1):
                    x2_copy(k, v + 1)
                adapter_inputs(k, v)
                low_rank(k, v)
                n = 2 * k + v
                dve.wait_ge(y_ps, n + 1)
                if not isinstance(k, int) or k > 0:
                    dve.wait_ge(y_stored[v], 16 * k)
                first, end = GROUPS_OF[1]
                nc.vector.tensor_copy(y_out[v][:, first:end], ps[2][:, HB:HB + end - first])
                dve.wait_ge(tail_out, n + 1)
                tail = y_out[v][:, T - TAIL:T]
                tt(tail, tail, ps[3][:, HB:HB + TAIL], ALU.add).then_inc(y_right, 1)

            x2_copy(0, 0)
            over_tiles(dve, tile)

        @block.tensor
        def _(pe):
            mm = nc.tensor.matmul
            PASSES = ((0, 0), (0, 1), (1, 0))

            def mixing(k, v):
                k, v = k + v // 2, v % 2
                n = 2 * k + v
                pe.wait_ge(x1_landed[v], 16 * k + 16)
                pe.wait_ge(gathered_m, n + 1)
                ready(pe, x2_copied, n)
                for i in range(K8):
                    ins = mm(ps[0][:, i * P:(i + 1) * P], x1_in[v][:, i * P:(i + 1) * P], m_gath[v][:], start=True, stop=True)
                ins.then_inc(x2_ps, 1)

            def turn(k, v):
                n = 2 * k + v
                pe.wait_ge(hrow_ready, n + 1)
                ready(pe, h_sum, n - 1)
                nc.tensor.transpose(ps[1][:, v * HB + P:v * HB + 2 * P], hrow[v][:], ident[:]).then_inc(h_turned, 1)

            def adapters(k, v):
                pe.wait_ge(c_landed[v], 64 * k + 64)
                pe.wait_ge(h2_ready, 2 * k + v + 1)
                mm(ps[1][0:KR, v * HB + 2 * P:v * HB + 3 * P], c_gath[v][:], hc[v][:], start=True, stop=True).then_inc(h_ps, 1)

            def dense(k, v):
                n = 2 * k + v
                outs = (ps[2][:, 0:GW], ps[2][:, HB:HB + GW], ps[3][:, 0:WT - 2 * GW])

                def group(g, chunks):
                    first, end = GROUPS_OF[g]
                    for i in chunks:
                        w = (dense0, dense1)[i // half_t]
                        for a, b in PASSES:
                            ins = mm(outs[g], x2t[v][:, a, i, :], w[:, b, i % half_t, first:end],
                                     start=i == a == b == 0, stop=g == 2 and i == K8 - 1 and a == 1)
                    return ins

                pe.wait_ge(x2_lo, n + 1)
                pe.wait_ge(a_lo, n + 1)
                ready(pe, hrow_ready, n)
                ready(pe, tail_out, n)
                group(2, range(K8)).then_inc(h2_ps, 1)
                ready(pe, y_left, n)
                group(0, range(K8))
                turn(k, v)
                ready(pe, y_right, n)
                group(1, range(half_t))
                adapters(k, v)
                group(1, range(half_t, K8))
                pe.wait_ge(h_lo, n + 1)
                pe.wait_ge(stack_landed[v], 64 * k + 64)
                for j, rows in ((0, 2 * KS), (1, KS + 2)):
                    for g, to in enumerate((outs[0], outs[1], ps[3][:, HB:HB + TAIL])):
                        first = GROUPS_OF[g][0]
                        end = min(GROUPS_OF[g][1], T)
                        ins = mm(to, hs[v][0:rows, j, :], stack[v][0:rows, j, first:end], start=g == 2 and j == 0, stop=j == 1)
                ins.then_inc(y_ps, 1)

            def tile(k, v):
                if exists(k, v + 1):
                    mixing(k, v + 1)
                dense(k, v)

            mixing(0, 0)
            over_tiles(pe, tile)


_INS = ["x", "itok_B_8_3872", "itok_B_0_15", "itok_B_6_15", "itok_B_0_2", "L0_cond_log_dt", "L0_cond_C",
        "L0_cond_log_A_real", "L0_cond_A_imag", "L0_cond_D", "L1_cond_weights", "L2_cond_base_weight",
        "L2_cond_base_bias", "L2_cond_lora_A_w", "L2_cond_lora_B_w", "L3_cond_W", "L3_cond_lora_A", "L3_cond_lora_B_w"]


def kernel(**inputs):
    import numpy as np
    from concourse import bacc
    from concourse.bass_utils import run_bass_kernel_spmd

    nc = bacc.Bacc("TRN2", target_bir_lowering=False, num_devices=1, dynamic_dma_scratch_size=1024)
    arrays, args = {}, []
    for name in _INS:
        a = np.ascontiguousarray(inputs[name])
        arrays[f"in_{name}"] = a
        args.append(nc.dram_tensor(f"in_{name}", a.shape, mybir.dt.from_np(a.dtype), kind="ExternalInput").ap())
    args.append(nc.dram_tensor("out_0", (B, C, T), F32, kind="ExternalOutput").ap())
    program(nc, *args)
    r = run_bass_kernel_spmd(nc, [arrays], core_ids=[0])
    return r.results[0]["out_0"]
```
